# Optimizing a Trainium2 kernel written in Bass

```python
import numpy as np
import jax
import jax.numpy as jnp

def _softmax(x, axis=-1):
    return jax.nn.softmax(x, axis=axis)

def _gelu(x):
    return jax.nn.gelu(x, approximate=True)

def _silu(x):
    return jax.nn.silu(x)

def _sigmoid(x):
    return jax.nn.sigmoid(x)

def _layernorm(x, axis=-1, eps=1e-05):
    m = jnp.mean(x, axis=axis, keepdims=True)
    v = jnp.var(x, axis=axis, keepdims=True)
    return (x - m) / jnp.sqrt(v + eps)

def _scatter_add(tgt, idx, src, axis=0):
    return tgt.at[idx].add(src)

def _segment_sum(src, seg, n):
    return jax.ops.segment_sum(src, seg, n)
kernel_name = 'mk_hybrid_d1_jaxref_r8_cfc63d'

def setup_inputs(seed: int=0):
    np.random.seed(seed)
    _w = jnp.asarray

    def _L0_attn_a_setup():
        import jax, jax.numpy as jnp
        import numpy as np
        B, T, C = (2, 256, 128)
        NH = 16
        HS = C // NH
        BD = max(HS // 4, 16)
        HORIZON = 64
        key = jax.random.key(seed)
        ks = jax.random.split(key, 10)
        s = 0.02
        return {'x': jax.random.normal(ks[0], (B, T, C), dtype=jnp.float32), 'W_disp': jax.random.normal(ks[1], (NH * BD, C), dtype=jnp.float32) * s, 'W_val': jax.random.normal(ks[2], (C, C), dtype=jnp.float32) * s, 'rel_pos_emb': jax.random.normal(ks[3], (HORIZON, BD), dtype=jnp.float32) * s, 'strain_fused_w': jax.random.normal(ks[4], (2 * BD, BD), dtype=jnp.float32) * s, 'strain_fused_b': jnp.zeros((2 * BD,), dtype=jnp.float32), 'pos_proj_w': jax.random.normal(ks[5], (BD, BD), dtype=jnp.float32) * s, 'bond_out_w': jax.random.normal(ks[6], (1, BD), dtype=jnp.float32) * s, 'damage_out_w': jax.random.normal(ks[7], (1, BD), dtype=jnp.float32) * s, 'damage_out_b': jnp.full((1,), -3.0, dtype=jnp.float32), 'c_proj_w': jax.random.normal(ks[8], (C, C), dtype=jnp.float32) * s}
    _L0_attn_a_in = _L0_attn_a_setup()

    def _L0_attn_b_setup():
        import jax, jax.numpy as jnp
        import numpy as np
        import math
        HIDDEN = 128
        NUM_LAYERS = 12
        LAYER_ID = 6
        BATCH = 8
        SEQ = 256
        NEG_INF = -1e+38

        def _wkv_full(k, v, w, u):
            B, T, H = k.shape
            kt = jnp.swapaxes(k, 0, 1)
            vt = jnp.swapaxes(v, 0, 1)

            def step(carry, kv):
                aa, bb, pp = carry
                k_t, v_t = kv
                ww = u + k_t
                p = jnp.maximum(pp, ww)
                e1 = jnp.exp(pp - p)
                e2 = jnp.exp(ww - p)
                wkv_t = (e1 * aa + e2 * v_t) / (e1 * bb + e2 + 1e-09)
                ww2 = w + pp
                p2 = jnp.maximum(ww2, k_t)
                e1b = jnp.exp(ww2 - p2)
                e2b = jnp.exp(k_t - p2)
                return ((e1b * aa + e2b * v_t, e1b * bb + e2b, p2), wkv_t)
            init = (jnp.zeros((B, H), k.dtype), jnp.zeros((B, H), k.dtype), jnp.full((B, H), NEG_INF, k.dtype))
            _, wkvs = jax.lax.scan(step, init, (kt, vt))
            return jnp.swapaxes(wkvs, 0, 1)
        key = jax.random.key(seed)
        ks = jax.random.split(key, 5)
        x = jax.random.normal(ks[0], (BATCH, SEQ, HIDDEN), dtype=jnp.float32)
        ratio_0_to_1 = LAYER_ID / max(NUM_LAYERS - 1, 1)
        h = np.arange(HIDDEN, dtype=np.float64)
        decay = -5.0 + 8.0 * (h / (HIDDEN - 1)) ** (0.7 + 1.3 * ratio_0_to_1)
        time_decay = jnp.asarray(decay, dtype=jnp.float32)
        time_first = jnp.full((HIDDEN,), math.log(0.3), dtype=jnp.float32)
        time_mix_k = jnp.full((1, 1, HIDDEN), 0.65, dtype=jnp.float32)
        time_mix_v = jnp.full((1, 1, HIDDEN), 0.45, dtype=jnp.float32)
        time_mix_r = jnp.full((1, 1, HIDDEN), 0.0, dtype=jnp.float32)
        scale = 0.02
        W_k = jax.random.normal(ks[1], (HIDDEN, HIDDEN), dtype=jnp.float32) * scale
        W_v = jax.random.normal(ks[2], (HIDDEN, HIDDEN), dtype=jnp.float32) * scale
        W_r = jax.random.normal(ks[3], (HIDDEN, HIDDEN), dtype=jnp.float32) * scale
        W_o = jax.random.normal(ks[4], (HIDDEN, HIDDEN), dtype=jnp.float32) * scale
        return {'x': x, 'time_decay': time_decay, 'time_first': time_first, 'time_mix_k': time_mix_k, 'time_mix_v': time_mix_v, 'time_mix_r': time_mix_r, 'W_k': W_k, 'W_v': W_v, 'W_r': W_r, 'W_o': W_o}
    _L0_attn_b_in = _L0_attn_b_setup()

    def _L0_ffn_setup():
        import jax, jax.numpy as jnp
        import numpy as np
        from jax import lax
        T, B, I, M, O = (32, 64, 128, 128, 128)

        def _xavier(key, shape):
            fan_out, fan_in = shape
            limit = float(np.sqrt(6.0 / (fan_in + fan_out)))
            return jax.random.uniform(key, shape, jnp.float32, -limit, limit)
        key = jax.random.key(seed)
        ks = jax.random.split(key, 9)
        x = jax.random.normal(ks[0], (T, B, I), jnp.float32)
        return {'x': x, 'wf': _xavier(ks[1], (M, I)), 'uf': _xavier(ks[2], (M, M)), 'bf': jnp.zeros((M,), jnp.float32), 'wi': _xavier(ks[3], (M, I)), 'ui': _xavier(ks[4], (M, M)), 'bi': jnp.zeros((M,), jnp.float32), 'wc': _xavier(ks[5], (M, I)), 'uc': _xavier(ks[6], (M, M)), 'bc': jnp.zeros((M,), jnp.float32), 'wo': _xavier(ks[7], (O, I)), 'uo': _xavier(ks[8], (O, M)), 'bo': jnp.zeros((O,), jnp.float32), 'in_c': jnp.zeros((M,), jnp.float32)}
    _L0_ffn_in = _L0_ffn_setup()
    _d = {'L0_attn_a_x': _L0_attn_a_in['x'], 'L0_attn_a_W_disp': _L0_attn_a_in['W_disp'], 'L0_attn_a_W_val': _L0_attn_a_in['W_val'], 'L0_attn_a_rel_pos_emb': _L0_attn_a_in['rel_pos_emb'], 'L0_attn_a_strain_fused_w': _L0_attn_a_in['strain_fused_w'], 'L0_attn_a_strain_fused_b': _L0_attn_a_in['strain_fused_b'], 'L0_attn_a_pos_proj_w': _L0_attn_a_in['pos_proj_w'], 'L0_attn_a_bond_out_w': _L0_attn_a_in['bond_out_w'], 'L0_attn_a_damage_out_w': _L0_attn_a_in['damage_out_w'], 'L0_attn_a_damage_out_b': _L0_attn_a_in['damage_out_b'], 'L0_attn_a_c_proj_w': _L0_attn_a_in['c_proj_w'], 'L0_attn_b_time_decay': _L0_attn_b_in['time_decay'], 'L0_attn_b_time_first': _L0_attn_b_in['time_first'], 'L0_attn_b_time_mix_k': _L0_attn_b_in['time_mix_k'], 'L0_attn_b_time_mix_v': _L0_attn_b_in['time_mix_v'], 'L0_attn_b_time_mix_r': _L0_attn_b_in['time_mix_r'], 'L0_attn_b_W_k': _L0_attn_b_in['W_k'], 'L0_attn_b_W_v': _L0_attn_b_in['W_v'], 'L0_attn_b_W_r': _L0_attn_b_in['W_r'], 'L0_attn_b_W_o': _L0_attn_b_in['W_o'], 'L0_ffn_wf': _L0_ffn_in['wf'], 'L0_ffn_uf': _L0_ffn_in['uf'], 'L0_ffn_bf': _L0_ffn_in['bf'], 'L0_ffn_wi': _L0_ffn_in['wi'], 'L0_ffn_ui': _L0_ffn_in['ui'], 'L0_ffn_bi': _L0_ffn_in['bi'], 'L0_ffn_wc': _L0_ffn_in['wc'], 'L0_ffn_uc': _L0_ffn_in['uc'], 'L0_ffn_bc': _L0_ffn_in['bc'], 'L0_ffn_wo': _L0_ffn_in['wo'], 'L0_ffn_uo': _L0_ffn_in['uo'], 'L0_ffn_bo': _L0_ffn_in['bo'], 'L0_ffn_in_c': _L0_ffn_in['in_c']}
    _x0 = _d['L0_attn_a_x']
    _d['L0_attn_a_x'] = jax.random.normal(jax.random.fold_in(jax.random.key(seed), 1), (8, 512, 128), dtype=_x0.dtype)
    del _x0
    return _d

def reference(L0_attn_a_x, L0_attn_a_W_disp, L0_attn_a_W_val, L0_attn_a_rel_pos_emb, L0_attn_a_strain_fused_w, L0_attn_a_strain_fused_b, L0_attn_a_pos_proj_w, L0_attn_a_bond_out_w, L0_attn_a_damage_out_w, L0_attn_a_damage_out_b, L0_attn_a_c_proj_w, L0_attn_b_time_decay, L0_attn_b_time_first, L0_attn_b_time_mix_k, L0_attn_b_time_mix_v, L0_attn_b_time_mix_r, L0_attn_b_W_k, L0_attn_b_W_v, L0_attn_b_W_r, L0_attn_b_W_o, L0_ffn_wf, L0_ffn_uf, L0_ffn_bf, L0_ffn_wi, L0_ffn_ui, L0_ffn_bi, L0_ffn_wc, L0_ffn_uc, L0_ffn_bc, L0_ffn_wo, L0_ffn_uo, L0_ffn_bo, L0_ffn_in_c):

    def _L0_attn_a_ref(x, W_disp, W_val, rel_pos_emb, strain_fused_w, strain_fused_b, pos_proj_w, bond_out_w, damage_out_w, damage_out_b, c_proj_w):
        import jax, jax.numpy as jnp
        import numpy as np
        B, T, C = (2, 256, 128)
        NH = 16
        HS = C // NH
        BD = max(HS // 4, 16)
        HORIZON = 64
        Bx, Tx, Cx = x.shape
        delta = min(HORIZON, Tx)
        gelu = lambda t: jax.nn.gelu(t, approximate=False)
        disp = (x @ W_disp.T).reshape(Bx, Tx, NH, BD).transpose(0, 2, 1, 3)
        val = (x @ W_val.T).reshape(Bx, Tx, NH, HS).transpose(0, 2, 1, 3)
        pad = ((0, 0), (0, 0), (delta - 1, 0), (0, 0))
        idx = jnp.arange(Tx)[:, None] + jnp.arange(delta)[None, :]
        disp_win = jnp.pad(disp, pad)[:, :, idx, :]
        strain = disp_win - disp[:, :, :, None, :]
        fused = strain @ strain_fused_w.T + strain_fused_b
        bond_feats, damage_feats = (fused[..., :BD], fused[..., BD:])
        pos_feat = rel_pos_emb[:delta] @ pos_proj_w.T
        bond_logits = (gelu(bond_feats + pos_feat) @ bond_out_w.T)[..., 0]
        damage = jax.nn.sigmoid((gelu(damage_feats) @ damage_out_w.T)[..., 0] + damage_out_b)
        logits = bond_logits - damage * 10.0
        cmask = jnp.arange(Tx)[:, None] - delta + 1 + jnp.arange(delta)[None, :] >= 0
        logits = jnp.where(cmask, logits, -jnp.inf)
        weights = jax.nn.softmax(logits, axis=-1)
        val_win = jnp.pad(val, pad)[:, :, idx, :]
        out = jnp.einsum('bhtw,bhtwd->bhtd', weights, val_win)
        out = out.transpose(0, 2, 1, 3).reshape(Bx, Tx, Cx)
        return out @ c_proj_w.T

    def _L0_attn_b_ref(x, time_decay, time_first, time_mix_k, time_mix_v, time_mix_r, W_k, W_v, W_r, W_o):
        import jax, jax.numpy as jnp
        import numpy as np
        import math
        HIDDEN = 128
        NUM_LAYERS = 12
        LAYER_ID = 6
        BATCH = 8
        SEQ = 256
        NEG_INF = -1e+38

        def _wkv_full(k, v, w, u):
            B, T, H = k.shape
            kt = jnp.swapaxes(k, 0, 1)
            vt = jnp.swapaxes(v, 0, 1)

            def step(carry, kv):
                aa, bb, pp = carry
                k_t, v_t = kv
                ww = u + k_t
                p = jnp.maximum(pp, ww)
                e1 = jnp.exp(pp - p)
                e2 = jnp.exp(ww - p)
                wkv_t = (e1 * aa + e2 * v_t) / (e1 * bb + e2 + 1e-09)
                ww2 = w + pp
                p2 = jnp.maximum(ww2, k_t)
                e1b = jnp.exp(ww2 - p2)
                e2b = jnp.exp(k_t - p2)
                return ((e1b * aa + e2b * v_t, e1b * bb + e2b, p2), wkv_t)
            init = (jnp.zeros((B, H), k.dtype), jnp.zeros((B, H), k.dtype), jnp.full((B, H), NEG_INF, k.dtype))
            _, wkvs = jax.lax.scan(step, init, (kt, vt))
            return jnp.swapaxes(wkvs, 0, 1)
        x_prev = jnp.pad(x[:, :-1, :], ((0, 0), (1, 0), (0, 0)))
        xk = x * time_mix_k + x_prev * (1.0 - time_mix_k)
        xv = x * time_mix_v + x_prev * (1.0 - time_mix_v)
        xr = x * time_mix_r + x_prev * (1.0 - time_mix_r)
        k = jnp.einsum('bth,oh->bto', xk, W_k)
        v = jnp.einsum('bth,oh->bto', xv, W_v)
        r = jax.nn.sigmoid(jnp.einsum('bth,oh->bto', xr, W_r))
        wkv = _wkv_full(k, v, time_decay, time_first)
        out = jnp.einsum('bth,oh->bto', r * wkv, W_o)
        return out

    def _L0_ffn_ref(x, wf, uf, bf, wi, ui, bi, wc, uc, bc, wo, uo, bo, in_c):
        import jax, jax.numpy as jnp
        import numpy as np
        from jax import lax
        T, B, I, M, O = (32, 64, 128, 128, 128)

        def _xavier(key, shape):
            fan_out, fan_in = shape
            limit = float(np.sqrt(6.0 / (fan_in + fan_out)))
            return jax.random.uniform(key, shape, jnp.float32, -limit, limit)
        batch = x.shape[1]
        c0 = jnp.broadcast_to(in_c, (batch, in_c.shape[0]))

        def step(c, xt):
            ft = jax.nn.sigmoid(xt @ wf.T + c @ uf.T + bf)
            it = jax.nn.sigmoid(xt @ wi.T + c @ ui.T + bi)
            gt = jnp.tanh(xt @ wc.T + c @ uc.T + bc)
            c = ft * c + it * gt
            return (c, None)
        c_final, _ = lax.scan(step, c0, x)
        h = jnp.tanh(jnp.einsum('tbi,oi->tbo', x, wo) + c_final @ uo.T + bo)
        return h
    x = L0_attn_a_x
    x = x + _L0_attn_a_ref(_layernorm(x, axis=-1), L0_attn_a_W_disp, L0_attn_a_W_val, L0_attn_a_rel_pos_emb, L0_attn_a_strain_fused_w, L0_attn_a_strain_fused_b, L0_attn_a_pos_proj_w, L0_attn_a_bond_out_w, L0_attn_a_damage_out_w, L0_attn_a_damage_out_b, L0_attn_a_c_proj_w)
    x = x + _L0_ffn_ref(_layernorm(x, axis=-1), L0_ffn_wf, L0_ffn_uf, L0_ffn_bf, L0_ffn_wi, L0_ffn_ui, L0_ffn_bi, L0_ffn_wc, L0_ffn_uc, L0_ffn_bc, L0_ffn_wo, L0_ffn_uo, L0_ffn_bo, L0_ffn_in_c)
    x = x + _L0_attn_b_ref(_layernorm(x, axis=-1), L0_attn_b_time_decay, L0_attn_b_time_first, L0_attn_b_time_mix_k, L0_attn_b_time_mix_v, L0_attn_b_time_mix_r, L0_attn_b_W_k, L0_attn_b_W_v, L0_attn_b_W_r, L0_attn_b_W_o)
    x = x + _L0_ffn_ref(_layernorm(x, axis=-1), L0_ffn_wf, L0_ffn_uf, L0_ffn_bf, L0_ffn_wi, L0_ffn_ui, L0_ffn_bi, L0_ffn_wc, L0_ffn_uc, L0_ffn_bc, L0_ffn_wo, L0_ffn_uo, L0_ffn_bo, L0_ffn_in_c)
    return x

_drawn_inputs = setup_inputs


def setup_inputs(seed=0):
    import zlib

    import numpy as np

    out = dict(_drawn_inputs(seed))
    spreads = {'L0_attn_a_strain_fused_b': (0.0, 0.8),
     'L0_attn_b_time_first': (-1.2039728164672852, 0.6),
     'L0_attn_b_time_mix_k': (0.6499999761581421, 0.6),
     'L0_attn_b_time_mix_v': (0.44999998807907104, 0.6),
     'L0_attn_b_time_mix_r': (0.0, 0.8),
     'L0_ffn_bf': (0.0, 0.498),
     'L0_ffn_bi': (0.0, 0.47),
     'L0_ffn_bc': (0.0, 0.1),
     'L0_ffn_bo': (0.0, 0.1),
     'L0_ffn_in_c': (0.0, 0.794)}
    factors = {'L0_attn_a_W_disp': 8.0,
     'L0_attn_a_W_val': 6.78,
     'L0_attn_a_rel_pos_emb': 8.0,
     'L0_attn_a_strain_fused_w': 8.0,
     'L0_attn_a_pos_proj_w': 24.048,
     'L0_attn_a_bond_out_w': 8.0,
     'L0_attn_a_damage_out_w': 8.0,
     'L0_attn_a_c_proj_w': 6.824,
     'L0_attn_b_time_decay': 6.869,
     'L0_attn_b_W_k': 8.0,
     'L0_attn_b_W_v': 5.242,
     'L0_attn_b_W_r': 8.0,
     'L0_attn_b_W_o': 5.173}
    for name, (base, spread) in spreads.items():
        noise = np.random.default_rng([zlib.crc32(name.encode()), seed]).standard_normal(out[name].shape)
        drawn = base * np.exp(spread * noise) if base else spread * noise
        out[name] = jnp.asarray(drawn.astype(out[name].dtype))
    for name, factor in factors.items():
        out[name] = (out[name] * factor).astype(out[name].dtype)
    return out
```

```python
from contextlib import ExitStack

import concourse.bass as bass
from concourse import mybir

F32 = mybir.dt.float32
BF16 = mybir.dt.bfloat16
ALU = mybir.AluOpType
ACT = mybir.ActivationFunctionType
AX_X = mybir.AxisListType.X

C = 128
B, T = 8, 512
NH, HS, BD = 16, 8, 16
W = 64
HU, BU = 4, 4
NF = 2 * BD
HG, BG = NH // HU, B // BU
UNITS = HG * BG
LQ = 4
NQ = W // LQ
SLOTS = W
TC = T // W
ND = 4
PAD = W
TP = T + PAD
MASKED = -1.0e38
NEG_INF = -1.0e38
EPS = 1.0e-5

TANH, COMBINE, MAXIMUM, SHIFT = 8, 11, 15, 19
EXPONENT = 25
TOTAL, NORMALISE = 28, 29
TURN, TURN_OUT = 33, 36
WEIGH, WEIGH_OUT = (50, 51, 55, 56), (53, 54, 58, 59)
PROJECT, ADD = (52, 53, 57, 58), (55, 56, 60, 61)
VALUES, VALUES_OUT = 2, 6


def pool_batches(s):
    if COMBINE <= s < SHIFT + 4:
        return 2
    return 1 if s % 3 == 0 else 2

NWIN = BU * TC

_COLS = [
    ("ident", 128), ("mean_w", 128), ("headmask", 128), ("fusedT", 128), ("disp", HG * 128),
    ("posT", 128), ("relT", W), ("place", LQ * 32), ("valT", 128),
    ("wf", 128), ("uf", 128), ("wi", 128), ("ui", 128), ("wc", 128), ("uc", 128), ("wo", 128), ("uo", 128),
    ("rk", 128), ("rv", 128), ("rr", 128), ("ro", 128),
    ("strain_b", 1), ("out_w", 1), ("damage_b", 1), ("eps", 1),
    ("bf", 1), ("bi", 1), ("bc", 1), ("bo", 1), ("c0", 1),
    ("td", 1), ("tf", 1), ("mk", 1), ("mv", 1), ("mr", 1),
    ("mask_place", 128), ("mask_rows", PAD + T),
]
COL, WIDTH = {}, 0
for _name, _n in _COLS:
    COL[_name] = (WIDTH, WIDTH + _n)
    WIDTH += _n


def program(nc, xT_dram, pack_dram, cp_dram, out_dram):
    logit_dram = nc.dram_tensor("logit_scratch", (UNITS, BU * 2 * HU, TC, W, W), F32, kind="Internal").ap()
    value_dram = nc.dram_tensor("value_scratch", (UNITS, C, NWIN, HU * HS), F32, kind="Internal").ap()
    with ExitStack() as ctx:
        def sb(name, shape, dt=F32):
            return ctx.enter_context(nc.sbuf_tensor(name, shape, dt))

        def sem(name):
            return ctx.enter_context(nc.semaphore(name))

        x = sb("residual", [128, B, T])
        xn = sb("xn", [128, B, TP])
        pack = sb("weights", [128, WIDTH])
        table = sb("table", [128, BU, TP])
        diff = sb("diff", [128, ND, BU, T])
        gelu = sb("gelu", [128, 2, BU, T])
        band = sb("band", [128, 3 * W - 1, W])
        side = sb("side", [128, 2 * W * W])
        value = sb("value", [128, NWIN, HU * HS])
        stage = sb("stage", [128, 2, T])
        attn = sb("attn", [128, 2, T])
        comb = sb("comb", [128, HG, 128])
        comb_u = sb("comb_u", [128, 128])
        cproj_u = sb("cproj_u", [128, 128])
        blockW = sb("blockW", [HU * BD, 128])
        posb = sb("posb", [128, W])
        outw = sb("outw", [128, LQ, 32])
        half_db = sb("half_db", [128, 1])
        mask_sel = sb("mask_sel", [LQ, 128], BF16)
        mask_rows = sb("mask_rows", [LQ, PAD + T], BF16)
        stat = sb("stat", [128, 3, W])

        psum = ctx.enter_context(nc.psum_tensor("psum", [128, 8, 512], F32))
        self_ps = psum[:, 0:BU, :]
        logit_ps = psum[:, 4:6, :]
        turn_ps = psum[:, 6:8, :]

        damage = side[:, 0:W * W].rearrange("p (w i) -> p w i", w=W)
        bandT = side[:, :].rearrange("p (i r) -> p i r", r=128)
        wpart = band[:, W:2 * W, :]

        def col(name, rows=128):
            a, b = COL[name]
            return pack[0:rows, a:b]

        s_load = sem("inputs_loaded")
        s_setup_v = sem("setup_by_vector")
        s_setup_p = sem("setup_by_gpsimd")
        s_setup_t = sem("setup_by_tensor")

        def layer_norm(tag):
            mean_ps, var_ps = psum[:, 0:2, :], psum[:, 2:4, :]
            square, std = gelu[:, 0, 0:2, :], gelu[:, 0, 2:4, :]
            mean_done, centred = sem(tag + "_mean_done"), sem(tag + "_centred")
            squared, var_done = sem(tag + "_squared"), sem(tag + "_var_done")
            std_done, rstd_done, normed = sem(tag + "_std_done"), sem(tag + "_rstd_done"), sem(tag + "_normed")
            with nc.Block() as block:
                @block.tensor
                def _(pe):
                    def mean(b):
                        if b >= 2:
                            pe.wait_ge(centred, b - 1)
                        pe.matmul(mean_ps[:, b % 2, :], col("mean_w"), x[:, b, :],
                                  start=True, stop=True).then_inc(mean_done, 1)

                    def var(b):
                        pe.wait_ge(squared, b + 1)
                        if b >= 2:
                            pe.wait_ge(std_done, b - 1)
                        pe.matmul(var_ps[:, b % 2, :], col("mean_w"), square[:, b % 2, :],
                                  start=True, stop=True).then_inc(var_done, 1)

                    mean(0)
                    for b in range(1, B):
                        mean(b)
                        var(b - 1)
                    var(B - 1)

                @block.scalar
                def _(act):
                    def root(b):
                        act.wait_ge(var_done, b + 1)
                        if b >= 2:
                            act.wait_ge(normed, b - 1)
                        act.activation(std[:, b % 2, :], var_ps[:, b % 2, :], ACT.Sqrt,
                                       bias=col("eps")).then_inc(std_done, 1)

                    for b in range(B):
                        act.wait_ge(centred, b + 1)
                        if b >= 2:
                            act.wait_ge(var_done, b - 1)
                        act.activation(square[:, b % 2, :], xn[:, b, PAD:], ACT.Square).then_inc(squared, 1)
                        if b >= 1:
                            root(b - 1)
                    root(B - 1)

                @block.vector
                def _(dve):
                    def scale(b):
                        dve.wait_ge(std_done, b + 1)
                        dve.reciprocal(std[:, b % 2, :], std[:, b % 2, :]).then_inc(rstd_done, 1)
                        dve.wait_ge(rstd_done, b + 1)
                        dve.tensor_tensor(xn[:, b, PAD:], xn[:, b, PAD:], std[:, b % 2, :],
                                          ALU.mult).then_inc(normed, 1)

                    for b in range(B):
                        dve.wait_ge(mean_done, b + 1)
                        dve.tensor_tensor(xn[:, b, PAD:], x[:, b, :], mean_ps[:, b % 2, :],
                                          ALU.subtract).then_inc(centred, 1)
                        if b >= 2:
                            scale(b - 2)
                    scale(B - 2)
                    scale(B - 1)
                    dve.wait_ge(normed, B)

        with nc.Block() as block:
            @block.sync
            def _(sp):
                sp.dma_start(pack[:, :], pack_dram).then_inc(s_load, 16)
                sp.dma_start(x[:, :, :], xT_dram).then_inc(s_load, 16)
                sp.wait_ge(s_load, 32)

            @block.gpsimd
            def _(pool):
                pool.memset(band[:, :, :], 0.0).then_inc(s_setup_p, 1)
                pool.memset(xn[:, :, 0:PAD], 0.0).then_inc(s_setup_p, 1)
                pool.memset(table[:, :, 0:PAD], 0.0).then_inc(s_setup_p, 1)
                pool.wait_ge(s_setup_p, 3)

            @block.vector
            def _(dve):
                dve.wait_ge(s_load, 32)
                dve.tensor_tensor(blockW[:, :], col("fusedT", HU * BD), col("headmask", HU * BD),
                                  ALU.mult).then_inc(s_setup_v, 1)
                dve.tensor_scalar(outw[:, :, :].rearrange("p l m -> p (l m)"), col("place"), col("out_w"), None,
                                  ALU.mult).then_inc(s_setup_v, 1)
                dve.tensor_scalar(half_db[:, :], col("damage_b"), 0.5, None, ALU.mult).then_inc(s_setup_v, 1)
                dve.tensor_copy(mask_sel[:, :], col("mask_place", LQ)).then_inc(s_setup_v, 1)
                dve.tensor_copy(mask_rows[:, :], col("mask_rows", LQ)).then_inc(s_setup_v, 1)
                dve.wait_ge(s_setup_t, 1)
                dve.tensor_copy(comb[:, :, :].rearrange("p g m -> p (g m)"), psum[:, 4, :]).then_inc(s_setup_v, 1)
                dve.tensor_scalar(posb[:, :], psum[:, 5, 0:W], col("strain_b"), None,
                                  ALU.add).then_inc(s_setup_v, 1)
                dve.wait_ge(s_setup_v, 7)

            @block.tensor
            def _(pe):
                pe.wait_ge(s_load, 32)
                pe.wait_ge(s_setup_v, 1)
                a = COL["disp"][0]
                for g in range(HG):
                    pe.matmul(psum[:, 4, g * 128:(g + 1) * 128], pack[0:HU * BD, a + g * 128:a + (g + 1) * 128],
                              blockW[:, :], start=True, stop=True)
                pe.matmul(psum[:, 5, 0:W], col("posT", BD), col("relT", BD),
                          start=True, stop=True).then_inc(s_setup_t, 1)

        layer_norm("ln_attention")
        attention(nc, sem, dict(locals()))
        layer_norm("ln_ffn1")
        ffn(nc, sem, "ffn1", dict(locals()))
        layer_norm("ln_rwkv")
        rwkv(nc, sem, dict(locals()))
        layer_norm("ln_ffn2")
        ffn(nc, sem, "ffn2", dict(locals()))

        s_out = sem("output_stored")
        with nc.Block() as block:
            @block.sync
            def _(sp):
                sp.dma_start(out_dram, x[:, :, :]).then_inc(s_out, 16)
                sp.wait_ge(s_out, 16)


def attention(nc, sem, m):
    x, xn, table, diff, gelu, band, value = (m[k] for k in ("x", "xn", "table", "diff", "gelu", "band", "value"))
    stage, attn, comb, comb_u, cproj_u, posb, outw = (
        m[k] for k in ("stage", "attn", "comb", "comb_u", "cproj_u", "posb", "outw"))
    self_ps, logit_ps, turn_ps, damage, bandT, wpart, stat = (
        m[k] for k in ("self_ps", "logit_ps", "turn_ps", "damage", "bandT", "wpart", "stat"))
    mask_sel, mask_rows, half_db, col = m["mask_sel"], m["mask_rows"], m["half_db"], m["col"]
    logit_dram, value_dram, cp_dram = m["logit_dram"], m["value_dram"], m["cp_dram"]

    comb_ready = sem("comb_ready")
    self_ready = sem("self_ready")
    table_ready = sem("table_ready")
    diff_by_vector = sem("diff_by_vector")
    diff_by_gpsimd = sem("diff_by_gpsimd")
    gelu_done = sem("gelu_done")
    reduced = sem("reduced")
    staged = sem("staged")
    written = [sem("written_even"), sem("written_odd")]
    reread = sem("reread")
    tanh_done = sem("tanh_done")
    combined = sem("combined")
    maxed = sem("maxed")
    shifted = sem("shifted")
    exped = sem("exped")
    summed = sem("summed")
    recip_done = sem("recip_done")
    probs = sem("probs")
    turned = sem("turned")
    turned_out = sem("turned_out")
    weighted = sem("weighted")
    weighted_out = sem("weighted_out")
    projected = sem("projected")
    added = sem("added")
    unit_weights = sem("unit_weights")
    values_done = sem("values_done")
    values_out = sem("values_out")
    values_stored = [sem("values_stored_even"), sem("values_stored_odd")]

    ci = W // 4

    def chunk(t3, c):
        return t3[:, :, c * ci:(c + 1) * ci]

    vstage = m["side"][:, 0:1024].rearrange("p (k n) -> p k n", k=2)

    with nc.Block() as block:
        @block.tensor
        def _(pe):
            def unit(u, produce, consume, first=False):
                def turn(g):
                    pe.wait_ge(probs, 4 * (u - 1) + g // 4 + 1)
                    if g >= 2:
                        pe.wait_ge(turned_out, 16 * (u - 1) + g - 1)
                    for k in range(4):
                        i = 4 * g + k
                        mm = pe.transpose(turn_ps[:, g % 2, k * 128:(k + 1) * 128],
                                          band[:, W - 1 - i:3 * W - 1 - i, i], col("ident"))
                    mm.then_inc(turned, 1)

                def weigh(b):
                    pe.wait_ge(turned_out, 16 * u)
                    pe.wait_ge(unit_weights, 32 * u)
                    if b >= 2:
                        pe.wait_ge(added, 4 * (u - 1) + b - 1)
                    for tc in range(TC):
                        for h in range(HU):
                            r = (b * HU + h) * TC + tc
                            mm = pe.matmul(turn_ps[32 * h:32 * h + HS, b % 2, tc * W:(tc + 1) * W],
                                           value[:, b * TC + tc, h * HS:(h + 1) * HS],
                                           bandT[:, :, r], start=True, stop=True, tile_position=(0, 32 * h))
                    mm.then_inc(weighted, 1)

                def project(b):
                    pe.wait_ge(weighted_out, 4 * (u - 1) + b + 1)
                    pe.matmul(turn_ps[:, b % 2, :], cproj_u[:, :], attn[:, b % 2, :],
                              start=True, stop=True).then_inc(projected, 1)

                def values(g):
                    if g >= 2:
                        pe.wait_ge(values_out, g - 1)
                    for k in range(4):
                        b, tc = (4 * g + k) // TC, (4 * g + k) % TC
                        mm = pe.matmul(turn_ps[:, g % 2, k * 128:(k + 1) * 128],
                                       xn[:, b, tc * W:tc * W + 2 * W], col("valT"), start=True, stop=True)
                    mm.then_inc(values_done, 1)

                def own_columns(v, b):
                    pe.matmul(self_ps[:, b, :], comb_u[:, :],
                              xn[:, bass.ds((v // HG) % BG * BU + b, 1), PAD:].rearrange("p a t -> p (a t)"),
                              start=True, stop=True).then_inc(self_ready, 1)

                if first:
                    pe.wait_ge(comb_ready, 1)
                    for b in range(BU):
                        own_columns(0, b)
                for s in range(SLOTS):
                    q, d, t0 = s // LQ, s % LQ, s // LQ * LQ
                    if produce:
                        pe.wait_ge(gelu_done, SLOTS * u + s + 1)
                        if d == 0:
                            if q >= 2 or not first:
                                pe.wait_ge(staged, NQ * u + q - 1)
                            pe.matmul(logit_ps[:, q % 2, :], mask_sel[:, :], mask_rows[:, PAD - t0:PAD - t0 + T],
                                      start=True, stop=False, skip_group_check=True)
                        for b in range(BU):
                            mm = pe.matmul(logit_ps[32 * b:32 * b + 32, q % 2, t0:], outw[:, d, :],
                                           gelu[:, s % 2, b, t0:], start=False, stop=(d == LQ - 1),
                                           tile_position=(0, 32 * b), skip_group_check=True)
                        mm.then_inc(reduced, 1)
                        if s == SLOTS - 4:
                            pe.wait_ge(comb_ready, u + 2)
                            pe.wait_ge(diff_by_vector, SLOTS * (u + 1))
                        if SLOTS - 4 <= s < SLOTS - 2:
                            for b in range(2 * (s - SLOTS + 4), 2 * (s - SLOTS + 4) + 2):
                                own_columns(u + 1, b)
                    if first and s >= VALUES and (s - VALUES) % 3 == 0 and (s - VALUES) // 3 < 16:
                        values((s - VALUES) // 3)
                    if consume:
                        if TURN <= s < TURN + 16:
                            turn(s - TURN)
                        if s in WEIGH:
                            weigh(WEIGH.index(s))
                        if s in PROJECT:
                            project(PROJECT.index(s))

            unit(0, True, False, first=True)
            with pe.Fori(1, UNITS) as u:
                unit(u, True, True)
            unit(UNITS, False, True)

        @block.scalar
        def _(act):
            def unit(u, produce, consume, first=False):
                for s in range(SLOTS):
                    t0 = s // LQ * LQ
                    if consume and TANH <= s < TANH + 4:
                        c = s - TANH
                        act.wait_ge(reread, 16 * 2 * BU * u)
                        act.activation(chunk(damage, c), chunk(damage, c), ACT.Tanh, bias=half_db[:, :],
                                       scale=0.5).then_inc(tanh_done, 1)
                    if consume and s == EXPONENT:
                        for k in range(2):
                            act.wait_ge(shifted, 4 * (u - 1) + 2 * k + 2)
                            h = wpart[:, :, 2 * k * ci:2 * (k + 1) * ci]
                            act.activation(h, h, ACT.Exp).then_inc(exped, 1)
                    if produce:
                        act.wait_ge(diff_by_vector, SLOTS * u + s + 1)
                        act.wait_ge(diff_by_gpsimd, SLOTS * u + s + 1)
                        if s >= 2 or not first:
                            act.wait_ge(reduced, SLOTS * u + s - 1)
                        act.activation(gelu[:, s % 2, :, t0:], diff[:, s % ND, :, t0:], ACT.Gelu,
                                       bias=posb[:, s:s + 1]).then_inc(gelu_done, 1)

            unit(0, True, False, first=True)
            with act.Fori(1, UNITS) as u:
                unit(u, True, True)
            unit(UNITS, False, True)

        @block.vector
        def _(dve):
            def unit(u, produce, consume, first=False):
                def stage_quad(q):
                    dve.wait_ge(reduced, SLOTS * u + LQ * (q + 1))
                    if q >= 2 or not first:
                        dve.wait_ge(written[q % 2], 16 * LQ * (NQ // 2 * u + (q // 2 if q >= 0 else -1)))
                    dve.tensor_copy(stage[:, q % 2, :], logit_ps[:, q % 2, :]).then_inc(staged, 1)

                def softmax(s):
                    step = next((k for k in (COMBINE, MAXIMUM, SHIFT, TOTAL) if k <= s < k + 4), None)
                    if step is None:
                        return
                    c = s - step
                    v = chunk(wpart, c)
                    mx, sm, rc = (stat[:, k, c * ci:(c + 1) * ci] for k in range(3))
                    if step == COMBINE:
                        dve.wait_ge(tanh_done, 4 * (u - 1) + c + 1)
                        dve.scalar_tensor_tensor(v, chunk(damage, c), -5.0, v, ALU.mult,
                                                 ALU.add).then_inc(combined, 1)
                    if step == MAXIMUM:
                        dve.wait_ge(combined, 4 * (u - 1) + c + 1)
                        dve.tensor_reduce(mx, v.rearrange("p w i -> p i w"), AX_X, ALU.max).then_inc(maxed, 1)
                    if step == SHIFT:
                        dve.wait_ge(maxed, 4 * (u - 1) + c + 1)
                        dve.tensor_tensor(v, v, mx.unsqueeze(1).broadcast_to([128, W, ci]),
                                          ALU.subtract).then_inc(shifted, 1)
                    if step == TOTAL:
                        dve.wait_ge(exped, 2 * (u - 1) + c // 2 + 1)
                        dve.tensor_reduce(sm, v.rearrange("p w i -> p i w"), AX_X, ALU.add).then_inc(summed, 1)
                        dve.wait_ge(summed, 4 * (u - 1) + c + 1)
                        dve.reciprocal(rc, sm).then_inc(recip_done, 1)

                def turn_out(g):
                    dve.wait_ge(turned, 16 * (u - 1) + g + 1)
                    dve.tensor_copy(bandT[:, 4 * g:4 * g + 4, :].rearrange("p i r -> p (i r)"),
                                    turn_ps[:, g % 2, :]).then_inc(turned_out, 1)

                def weigh_out(b):
                    dve.wait_ge(weighted, 4 * (u - 1) + b + 1)
                    dve.tensor_copy(attn[:, b % 2, :], turn_ps[:, b % 2, :]).then_inc(weighted_out, 1)

                def add(b):
                    dve.wait_ge(projected, 4 * (u - 1) + b + 1)
                    xb = x[:, bass.ds(((u - 1) // HG) * BU + b, 1), :].rearrange("p a t -> p (a t)")
                    dve.tensor_tensor(xb, xb, turn_ps[:, b % 2, :], ALU.add).then_inc(added, 1)

                def values_out_(g):
                    dve.wait_ge(values_done, g + 1)
                    if g >= 2:
                        dve.wait_ge(values_stored[g % 2], 16 * HG * (g // 2))
                    dve.tensor_copy(vstage[:, g % 2, :], turn_ps[:, g % 2, :]).then_inc(values_out, 1)

                if produce:
                    if first:
                        dve.tensor_copy(comb_u[:, :], comb[:, 0, :]).then_inc(comb_ready, 1)
                    for b in range(BU):
                        dve.wait_ge(self_ready, 4 * u + b + 1)
                        if not first and b == 0:
                            dve.wait_ge(diff_by_gpsimd, SLOTS * u)
                            dve.wait_ge(diff_by_vector, SLOTS * u)
                        dve.tensor_copy(table[:, b, PAD:], self_ps[:, b, :]).then_inc(table_ready, 1)
                    dve.wait_ge(table_ready, 4 * u + 4)
                for s in range(SLOTS):
                    q, d, t0 = s // LQ, s % LQ, s // LQ * LQ
                    if produce:
                        nb = BU - pool_batches(s)
                        if s >= ND or not first:
                            dve.wait_ge(gelu_done, SLOTS * u + s - ND + 1)
                        dve.tensor_tensor(diff[:, s % ND, 0:nb, t0:], table[:, 0:nb, PAD + t0 - s:TP - s],
                                          self_ps[:, 0:nb, t0:], ALU.subtract).then_inc(diff_by_vector, 1)
                        if d == 3 and q > 0:
                            stage_quad(q - 1)
                    if d == 3 and q == 0 and consume:
                        stage_quad(-1)
                    if first and s >= VALUES_OUT and (s - VALUES_OUT) % 3 == 0 and (s - VALUES_OUT) // 3 < 16:
                        values_out_((s - VALUES_OUT) // 3)
                    if produce and s == 48:
                        dve.tensor_copy(comb_u[:, :], comb[:, bass.ds((u + 1) % HG, 1), :].rearrange(
                            "p a m -> p (a m)")).then_inc(comb_ready, 1)
                    if consume:
                        softmax(s)
                        if TURN_OUT <= s < TURN_OUT + 16:
                            turn_out(s - TURN_OUT)
                        if s in WEIGH_OUT:
                            weigh_out(WEIGH_OUT.index(s))
                        if s in ADD:
                            add(ADD.index(s))

            unit(0, True, False, first=True)
            with dve.Fori(1, UNITS) as u:
                unit(u, True, True)
            unit(UNITS, False, True)
            dve.wait_ge(added, 4 * UNITS)

        @block.gpsimd
        def _(pool):
            def unit(u, produce, consume, first=False):
                if produce:
                    pool.wait_ge(table_ready, 4 * u + 4)
                for s in range(SLOTS):
                    d, t0 = s % LQ, s // LQ * LQ
                    if produce:
                        nb = BU - pool_batches(s)
                        if s >= ND or not first:
                            pool.wait_ge(gelu_done, SLOTS * u + s - ND + 1)
                        pool.tensor_tensor(diff[:, s % ND, nb:, t0:], table[:, nb:, PAD + t0 - s:TP - s],
                                           table[:, nb:, PAD + t0:], ALU.subtract).then_inc(diff_by_gpsimd, 1)
                    if consume and NORMALISE <= s < NORMALISE + 8 and (s - NORMALISE) % 2 == 0:
                        c = (s - NORMALISE) // 2
                        v = chunk(wpart, c)
                        pool.wait_ge(recip_done, 4 * (u - 1) + c + 1)
                        pool.tensor_tensor(v, v, stat[:, 2, c * ci:(c + 1) * ci].unsqueeze(1).broadcast_to(
                            [128, W, ci]), ALU.mult).then_inc(probs, 1)

            unit(0, True, False, first=True)
            with pool.Fori(1, UNITS) as u:
                unit(u, True, True)
            unit(UNITS, False, True)

        @block.sync
        def _(sp):
            def unit(u, produce, consume, first=False):
                def write(q):
                    sp.wait_ge(staged, NQ * u + q + 1)
                    v, qq = (u, q) if q >= 0 else (u - 1, NQ - 1)
                    for w in range(LQ):
                        dst = logit_dram[bass.ds(v, 1), :, :, W - LQ * (qq + 1) + w, :].rearrange(
                            "a r c i -> (a r) c i")
                        src = stage[w:128:LQ, q % 2, :].rearrange("r (c i) -> r c i", i=W)
                        sp.dma_start(dst, src).then_inc(written[q % 2], 16)

                def read():
                    sp.wait_ge(written[0], 16 * LQ * NQ // 2 * u)
                    sp.wait_ge(written[1], 16 * LQ * NQ // 2 * u)
                    for b in range(BU):
                        for kind, dst in ((0, wpart), (1, damage)):
                            r = (b * 2 + kind) * HU
                            src = logit_dram[bass.ds(u - 1, 1), r:r + HU, :, :, :].rearrange(
                                "a h c w i -> (a h c) w i")
                            sp.dma_start(dst[32 * b:32 * b + 32, :, :], src).then_inc(reread, 16)

                def weights():
                    sp.dma_start(cproj_u[:, :], cp_dram[bass.ds((u - 1) % HG, 1), :, :].rearrange(
                        "a p m -> (a p) m")).then_inc(unit_weights, 16)
                    sp.dma_start(value[:, :, :], value_dram[bass.ds(u - 1, 1), :, :, :].rearrange(
                        "a p n d -> (a p) n d")).then_inc(unit_weights, 16)

                def store_values(g):
                    sp.wait_ge(values_out, g + 1)
                    bg, n0 = (4 * g) // NWIN, (4 * g) % NWIN
                    for hg in range(HG):
                        src = vstage[:, g % 2, :].rearrange("p (k n) -> p k n", k=4)[:, :, hg * 32:(hg + 1) * 32]
                        sp.dma_start(value_dram[bg * HG + hg, :, n0:n0 + 4, :], src).then_inc(
                            values_stored[g % 2], 16)

                for q in range(NQ):
                    if q > 0:
                        if produce:
                            write(q - 1)
                    elif consume:
                        write(-1)
                        read()
                        weights()
                    if first:
                        for g in range(16):
                            if (3 * g + VALUES_OUT) // LQ == q:
                                store_values(g)
                if first:
                    for k in range(2):
                        sp.wait_ge(values_stored[k], 16 * HG * 8)

            unit(0, True, False, first=True)
            with sp.Fori(1, UNITS) as u:
                unit(u, True, True)
            unit(UNITS, False, True)
            for k in range(2):
                sp.wait_ge(written[k], 16 * LQ * NQ // 2 * UNITS)


def ffn(nc, sem, tag, m):
    x, xn, psum, col, band, side, pack = (m[k] for k in ("x", "xn", "psum", "col", "band", "side", "pack"))
    flat = band[:, :, :].rearrange("p a b -> p (a b)")
    HALF = T // 2
    state = flat[:, 0:2 * T].rearrange("p (k t) -> p k t", k=2)
    gates = flat[:, 2 * T:5 * T].rearrange("p (g t) -> p g t", g=3)
    prod = flat[:, 5 * T:7 * T].rearrange("p (g t) -> p g t", g=2)
    out = flat[:, 7 * T:9 * T].rearrange("p (k t) -> p k t", k=2)
    rec = flat[:, 9 * T:10 * T].rearrange("p (g m) -> p g m", g=4)
    bias = flat[:, 10 * T:10 * T + 4]
    ready = sem(tag + "_weights_ready")
    z = sem(tag + "_z")
    gated = sem(tag + "_gated")
    prods = sem(tag + "_products")
    stepped = sem(tag + "_stepped")
    fin = sem(tag + "_output_z")
    fin_act = sem(tag + "_output_tanh")
    fin_add = sem(tag + "_output_added")
    weights = (("wf", 0), ("wi", 1), ("wc", 2))
    zbank = [[psum[:, 3 * k + g, 0:HALF] for g in range(3)] for k in range(2)]
    with nc.Block() as block:
        @block.tensor
        def _(pe):
            pe.wait_ge(ready, 8)

            def inputs(b, k):
                if b:
                    pe.wait_ge(gated, 6 * (b - 1) + 3 * k + 3)
                for name, g in weights:
                    pe.matmul(zbank[k][g], col(name), xn[:, b, PAD + k * HALF:PAD + (k + 1) * HALF],
                              start=True, stop=False, skip_group_check=True)

            def recur(b, k):
                if b:
                    pe.wait_ge(stepped, 2 * (b - 1) + k + 1)
                for g in range(3):
                    pe.matmul(zbank[k][g], rec[:, g, :], state[:, b % 2, k * HALF:(k + 1) * HALF],
                              start=False, stop=True, skip_group_check=True).then_inc(z, 1)

            for k in range(2):
                inputs(0, k)
            for b in range(B):
                for k in range(2):
                    recur(b, k)
                    if b + 1 < B and k:
                        inputs(b + 1, 0)
                if b + 1 < B:
                    inputs(b + 1, 1)
            pe.wait_ge(stepped, 2 * B)
            for b in range(B):
                if b >= 2:
                    pe.wait_ge(fin_act, b - 1)
                pe.matmul(psum[:, 6 + b % 2, :], col("wo"), xn[:, b, PAD:], start=True, stop=False)
                pe.matmul(psum[:, 6 + b % 2, :], rec[:, 3, :], state[:, B % 2, :],
                          start=False, stop=True).then_inc(fin, 1)

        @block.scalar
        def _(act):
            act.wait_ge(ready, 8)
            for b in range(B):
                for k in range(2):
                    h = slice(k * HALF, (k + 1) * HALF)
                    for g in range(3):
                        act.wait_ge(z, 6 * b + 3 * k + g + 1)
                        if b:
                            act.wait_ge(prods, 4 * (b - 1) + 2 * k + 2)
                        act.activation(gates[:, g, h], zbank[k][g], ACT.Tanh,
                                       bias=bias[:, g:g + 1], scale=0.5 if g < 2 else 1.0).then_inc(gated, 1)
            for b in range(B):
                act.wait_ge(fin, b + 1)
                if b >= 2:
                    act.wait_ge(fin_add, b - 1)
                act.activation(out[:, b % 2, :], psum[:, 6 + b % 2, :], ACT.Tanh,
                               bias=col("bo")).then_inc(fin_act, 1)

        @block.vector
        def _(dve):
            for g, name in enumerate(("uf", "ui", "uc", "uo")):
                dve.tensor_scalar(rec[:, g, :], col(name), 0.5, None, ALU.mult).then_inc(ready, 1)
            dve.tensor_scalar(bias[:, 0:1], col("bf"), 0.5, None, ALU.mult).then_inc(ready, 1)
            dve.tensor_scalar(bias[:, 1:2], col("bi"), 0.5, None, ALU.mult).then_inc(ready, 1)
            dve.tensor_copy(bias[:, 2:3], col("bc")).then_inc(ready, 1)
            dve.tensor_scalar(state[:, 0, :], col("c0").broadcast_to([128, T]), 2.0, None,
                              ALU.mult).then_inc(ready, 1)
            dve.wait_ge(ready, 8)
            for b in range(B):
                for k in range(2):
                    h = slice(k * HALF, (k + 1) * HALF)
                    if b:
                        dve.wait_ge(stepped, 2 * (b - 1) + k + 1)
                    dve.wait_ge(gated, 6 * b + 3 * k + 1)
                    dve.scalar_tensor_tensor(prod[:, 0, h], gates[:, 0, h], 1.0, state[:, b % 2, h],
                                             ALU.add, ALU.mult).then_inc(prods, 1)
                    dve.wait_ge(gated, 6 * b + 3 * k + 3)
                    dve.scalar_tensor_tensor(prod[:, 1, h], gates[:, 1, h], 1.0, gates[:, 2, h],
                                             ALU.add, ALU.mult).then_inc(prods, 1)
                    dve.wait_ge(prods, 4 * b + 2 * k + 2)
                    dve.wait_ge(z, 6 * b + 3 * k + 3)
                    dve.scalar_tensor_tensor(state[:, (b + 1) % 2, h], prod[:, 0, h], 0.5, prod[:, 1, h],
                                             ALU.mult, ALU.add).then_inc(stepped, 1)
            for b in range(B):
                dve.wait_ge(fin_act, b + 1)
                dve.tensor_tensor(x[:, b, :], x[:, b, :], out[:, b % 2, :], ALU.add).then_inc(fin_add, 1)
            dve.wait_ge(fin_add, B)


def rwkv(nc, sem, m):
    x, xn, psum, col, band, side, diff, gelu = (
        m[k] for k in ("x", "xn", "psum", "col", "band", "side", "diff", "gelu"))
    flat = band[:, :, :].rearrange("p a b -> p (a b)")
    region = [flat[:, k * 528:(k + 1) * 528] for k in range(23)]
    region += [side[:, k * 528:(k + 1) * 528] for k in range(15)]
    free = iter(range(38))

    def two(width=T):
        a, b = region[next(free)], region[next(free)]
        return [a[:, 0:width], b[:, 0:width]]

    delta = two()
    mixed = {n: two() for n in "kvr"}
    mp = two(T + 1)
    aa, bb = two(T + 1), two(T + 1)
    e1b, e2b = two(), two()
    ev = two()
    p = two()
    e1, e2 = two(), two()
    num, den = two(), two()
    gate = two()
    init = sem("rwkv_init")
    deltas = sem("rwkv_delta")
    mixed_done = sem("rwkv_mixed")
    kvr = sem("rwkv_kvr")
    v_step = sem("rwkv_vector")
    exps = sem("rwkv_exps")
    wo_done = sem("rwkv_out")
    out_added = sem("rwkv_added")
    scan_args = sem("rwkv_scan_args")
    read_args = sem("rwkv_read_args")
    gated = sem("rwkv_gated")
    with nc.Block() as block:
        @block.tensor
        def _(pe):
            def out(b):
                pe.wait_ge(gated, b + 1)
                if b >= 2:
                    pe.wait_ge(out_added, b - 1)
                pe.matmul(psum[:, 6 + b % 2, :], col("ro"), num[b % 2], start=True, stop=True).then_inc(wo_done, 1)

            for b in range(B):
                for j, (n, w) in enumerate((("k", "rk"), ("v", "rv"), ("r", "rr"))):
                    pe.wait_ge(mixed_done, 3 * b + j + 1)
                    if b >= 2 and j == 0:
                        pe.wait_ge(gated, b - 1)
                    pe.matmul(psum[:, 3 * (b % 2) + j, :], col(w), mixed[n][b % 2],
                              start=True, stop=True).then_inc(kvr, 1)
                if b:
                    out(b - 1)
            out(B - 1)

        @block.scalar
        def _(act):
            for b in range(B):
                k = b % 2
                act.wait_ge(kvr, 3 * b + 3)
                if b >= 2:
                    act.wait_ge(gated, b - 1)
                act.activation(gate[k], psum[:, 3 * k + 2, :], ACT.Tanh, scale=0.5).then_inc(exps, 1)
                for j, t in enumerate((e1b, e2b)):
                    act.wait_ge(scan_args, 2 * b + j + 1)
                    act.activation(t[k], t[k], ACT.Exp).then_inc(exps, 1)
                for j, t in enumerate((e1, e2)):
                    act.wait_ge(read_args, 2 * b + j + 1)
                    act.activation(t[k], t[k], ACT.Exp).then_inc(exps, 1)

        @block.gpsimd
        def _(pool):
            for k in range(2):
                pool.memset(mp[k][:, 0:1], NEG_INF).then_inc(init, 1)
                pool.memset(aa[k][:, 0:1], 0.0).then_inc(init, 1)
                pool.memset(bb[k][:, 0:1], 0.0).then_inc(init, 1)
            for b in range(B):
                k = b % 2
                cur, prev = xn[:, b, PAD:], xn[:, b, PAD - 1:TP - 1]
                if b >= 2:
                    pool.wait_ge(mixed_done, 3 * (b - 1))
                pool.tensor_tensor(delta[k], cur, prev, ALU.subtract).then_inc(deltas, 1)

        @block.vector
        def _(dve):
            dve.wait_ge(init, 6)
            count = [0]

            def then(ins, *waits):
                count[0] += 1
                ins.then_inc(v_step, 1)

            def own():
                dve.wait_ge(v_step, count[0])

            def mix(b):
                k = b % 2
                prev = xn[:, b, PAD - 1:TP - 1]
                dve.wait_ge(deltas, b + 1)
                for j, (n, w) in enumerate((("k", "mk"), ("v", "mv"), ("r", "mr"))):
                    if b >= 2:
                        dve.wait_ge(kvr, 3 * (b - 2) + j + 1)
                    dve.scalar_tensor_tensor(mixed[n][k], delta[k], col(w), prev, ALU.mult,
                                             ALU.add).then_inc(mixed_done, 1)

            mix(0)
            for b in range(B):
                k = b % 2
                kk, vv = psum[:, 3 * k, :], psum[:, 3 * k + 1, :]
                if b + 1 < B:
                    mix(b + 1)
                dve.wait_ge(kvr, 3 * b + 3)
                if b >= 2:
                    dve.wait_ge(wo_done, b - 1)
                then(dve.tensor_tensor_scan(mp[k][:, 1:T + 1], col("td").broadcast_to([128, T]), kk, NEG_INF,
                                            ALU.add, ALU.max))
                own()
                before, after = mp[k][:, 0:T], mp[k][:, 1:T + 1]
                dve.scalar_tensor_tensor(e1b[k], before, col("td"), after, ALU.add,
                                         ALU.subtract).then_inc(scan_args, 1)
                dve.tensor_tensor(e2b[k], kk, after, ALU.subtract).then_inc(scan_args, 1)
                then(dve.scalar_tensor_tensor(p[k], kk, col("tf"), before, ALU.add, ALU.max))
                own()
                dve.tensor_tensor(e1[k], before, p[k], ALU.subtract).then_inc(read_args, 1)
                dve.scalar_tensor_tensor(e2[k], kk, col("tf"), p[k], ALU.add, ALU.subtract).then_inc(read_args, 1)
                dve.wait_ge(exps, 5 * b + 3)
                then(dve.tensor_tensor(ev[k], e2b[k], vv, ALU.mult))
                then(dve.tensor_tensor_scan(bb[k][:, 1:T + 1], e1b[k], e2b[k], 0.0, ALU.mult, ALU.add))
                own()
                then(dve.tensor_tensor_scan(aa[k][:, 1:T + 1], e1b[k], ev[k], 0.0, ALU.mult, ALU.add))
                dve.wait_ge(exps, 5 * b + 5)
                then(dve.tensor_tensor(den[k], e1[k], bb[k][:, 0:T], ALU.mult))
                own()
                then(dve.tensor_tensor(num[k], e1[k], aa[k][:, 0:T], ALU.mult))
                then(dve.scalar_tensor_tensor(den[k], e2[k], 1.0e-9, den[k], ALU.add, ALU.add))
                own()
                then(dve.tensor_tensor(e2[k], e2[k], vv, ALU.mult))
                then(dve.reciprocal(den[k], den[k]))
                own()
                then(dve.tensor_tensor(num[k], num[k], e2[k], ALU.add))
                own()
                then(dve.tensor_tensor(num[k], num[k], den[k], ALU.mult))
                then(dve.tensor_scalar(gate[k], gate[k], 0.5, 0.5, ALU.mult, ALU.add))
                own()
                dve.tensor_tensor(num[k], num[k], gate[k], ALU.mult).then_inc(gated, 1)
                if b:
                    dve.wait_ge(wo_done, b)
                    dve.tensor_tensor(x[:, b - 1, :], x[:, b - 1, :], psum[:, 6 + (b - 1) % 2, :],
                                      ALU.add).then_inc(out_added, 1)
            dve.wait_ge(wo_done, B)
            dve.tensor_tensor(x[:, B - 1, :], x[:, B - 1, :], psum[:, 6 + (B - 1) % 2, :],
                              ALU.add).then_inc(out_added, 1)
            dve.wait_ge(out_added, B)


def kernel(**inputs):
    import numpy as np
    import concourse.bacc as bacc
    from concourse.bass_utils import run_bass_kernel_spmd as run

    A = {k: np.asarray(v) for k, v in inputs.items()}
    a = {k[len("L0_attn_a_"):]: v for k, v in A.items() if k.startswith("L0_attn_a_")}
    r = {k[len("L0_attn_b_"):]: v for k, v in A.items() if k.startswith("L0_attn_b_")}
    f = {k[len("L0_ffn_"):]: v for k, v in A.items() if k.startswith("L0_ffn_")}

    headmask = np.kron(np.eye(HU, dtype=np.float32), np.ones((BD, NF), np.float32))
    place = np.zeros((HU, 2, BD, LQ, 2, HU, LQ), np.float32)
    for h in range(HU):
        for kind in range(2):
            for lag in range(LQ):
                place[h, kind, :, lag, kind, h, LQ - 1 - lag] = 1.0
    mask_place = np.zeros((LQ, BU, 2, HU, LQ), np.float32)
    mask_rows = np.zeros((LQ, PAD + T), np.float32)
    for w in range(LQ):
        mask_place[w, :, 0, :, w] = 1.0
        mask_rows[w, :PAD + LQ - 1 - w] = MASKED

    def columns(v, n=1):
        return np.tile(np.asarray(v).reshape(-1, 1), (n, 1))

    parts = {
        "ident": np.eye(128, dtype=np.float32),
        "mean_w": np.full((128, 128), 1.0 / C, np.float32),
        "headmask": headmask,
        "fusedT": np.tile(a["strain_fused_w"].T, (HU, HU)),
        "disp": a["W_disp"].reshape(HG, HU * BD, C).transpose(1, 0, 2).reshape(HU * BD, HG * C),
        "posT": np.tile(np.concatenate([a["pos_proj_w"].T, np.zeros((BD, BD), np.float32)], 1), (1, HU)),
        "relT": a["rel_pos_emb"][::-1].T,
        "place": place.reshape(128, LQ * 32),
        "valT": a["W_val"].T,
        "wf": f["wf"].T, "uf": f["uf"].T, "wi": f["wi"].T, "ui": f["ui"].T,
        "wc": f["wc"].T, "uc": f["uc"].T, "wo": f["wo"].T, "uo": f["uo"].T,
        "rk": r["W_k"].T, "rv": r["W_v"].T, "rr": r["W_r"].T, "ro": r["W_o"].T,
        "strain_b": columns(a["strain_fused_b"], HU),
        "out_w": columns(np.concatenate([a["bond_out_w"][0], a["damage_out_w"][0]]), HU),
        "damage_b": columns(a["damage_out_b"], 128),
        "eps": np.full((128, 1), EPS, np.float32),
        "bf": columns(f["bf"]), "bi": columns(f["bi"]), "bc": columns(f["bc"]), "bo": columns(f["bo"]),
        "c0": columns(f["in_c"]),
        "td": columns(r["time_decay"]), "tf": columns(r["time_first"]),
        "mk": columns(r["time_mix_k"]), "mv": columns(r["time_mix_v"]), "mr": columns(r["time_mix_r"]),
        "mask_place": mask_place.reshape(LQ, 128), "mask_rows": mask_rows,
    }
    pack = np.zeros((128, WIDTH), np.float32)
    for name, part in parts.items():
        lo, hi = COL[name]
        pack[:part.shape[0], lo:hi] = part
    cp = np.zeros((HG, HU, 32, C), np.float32)
    cp[:, :, :HS, :] = a["c_proj_w"].T.reshape(HG, HU, HS, C)
    xT = np.ascontiguousarray(a["x"].transpose(2, 0, 1))

    nc = bacc.Bacc("TRN2", target_bir_lowering=False, num_devices=1)
    arrays = {"xT": xT, "pack": pack, "cp": cp.reshape(HG, 128, C)}
    args = [nc.dram_tensor(k, v.shape, mybir.dt.from_np(v.dtype), kind="ExternalInput").ap()
            for k, v in arrays.items()]
    args.append(nc.dram_tensor("outT", (128, B, T), F32, kind="ExternalOutput").ap())
    program(nc, *args)
    res = run(nc, [arrays], core_ids=[0])
    return np.ascontiguousarray(res.results[0]["outT"].transpose(1, 2, 0))
```

```python
from contextlib import ExitStack

import concourse.bass as bass
from concourse import mybir

F32 = mybir.dt.float32
BF16 = mybir.dt.bfloat16
ALU = mybir.AluOpType
ACT = mybir.ActivationFunctionType
AX_X = mybir.AxisListType.X

C = 128
B, T = 8, 512
NH, HS, BD = 16, 8, 16
W = 64
HU, BU = 4, 4
NF = 2 * BD
HG, BG = NH // HU, B // BU
UNITS = HG * BG
LQ = 4
NQ = W // LQ
SLOTS = W
TC = T // W
ND = 4
PAD = W
TP = T + PAD
MASKED = -1.0e38
NEG_INF = -1.0e38
EPS = 1.0e-5

TANH, COMBINE, MAXIMUM, SHIFT = 12, 15, 19, 23
EXPONENT = 28
TOTAL, NORMALISE = 31, 32
TURN, TURN_OUT = 35, 38
WEIGH, WEIGH_OUT = (52, 53, 56, 57), (55, 56, 59, 60)
PROJECT, ADD = (54, 55, 58, 59), (57, 58, 61, 62)
VALUES, VALUES_OUT = 2, 6
NEXT_G = 48
NEXT_ORDER = (3, 2, 1, 0)


def share_differences():
    shares, vector, gpsimd = [], 0.0, 0.0
    for s in range(SLOTS):
        vector += 1.8 * (COMBINE <= s < SHIFT + 4 or TOTAL <= s < TOTAL + 4)
        vector += (s % LQ == 3) + (TURN_OUT <= s < TURN_OUT + 16) + (s in WEIGH_OUT) + (s in ADD)
        gpsimd += 3.6 * (s in range(NORMALISE, NORMALISE + 8, 2))
        n = 2 if vector + (BU - 1) > gpsimd + 3.0 else 1
        vector, gpsimd = vector + BU - n, gpsimd + 2.05 * n
        shares.append(n)
    return shares


POOL_BATCHES = share_differences()
NWIN = BU * TC

_COLS = [
    ("ident", 128), ("mean_w", 1), ("centre_w", 128), ("ones_w", 128), ("minus_half", 4), ("headmask", 128), ("fusedT", 128), ("disp", HG * 128),
    ("posT", 128), ("relT", W), ("place", LQ * 32), ("valT", 128),
    ("wf", 128), ("uf", 128), ("wi", 128), ("ui", 128), ("wc", 128), ("uc", 128), ("wo", 128), ("uo", 128),
    ("rk", 128), ("rv", 128), ("rr", 128), ("ro", 128),
    ("strain_b", 1), ("out_w", 1), ("damage_b", 1),
    ("bf", 1), ("bi", 1), ("bc", 1), ("bo", 1), ("c0", 1),
    ("td", 1), ("tf", 1), ("mk", 1), ("mv", 1), ("mr", 1),
    ("mask_place", 128), ("mask_rows", PAD + T),
]
COL, WIDTH = {}, 0
for _name, _n in _COLS:
    COL[_name] = (WIDTH, WIDTH + _n)
    WIDTH += _n


def program(nc, xT_dram, pack_dram, cp_dram, out_dram):
    logit_dram = nc.dram_tensor("logit_scratch", (UNITS, BU * 2 * HU, TC, W, W), F32, kind="Internal").ap()
    value_dram = nc.dram_tensor("value_scratch", (UNITS, C, NWIN, HU * HS), F32, kind="Internal").ap()
    with ExitStack() as ctx:
        def sb(name, shape, dt=F32):
            return ctx.enter_context(nc.sbuf_tensor(name, shape, dt))

        def sem(name):
            return ctx.enter_context(nc.semaphore(name))

        x = sb("residual", [128, B, T])
        xn = sb("xn", [128, B, TP])
        pack = sb("weights", [128, WIDTH])
        table = sb("table", [128, BU, TP])
        diff = sb("diff", [128, ND, BU, T])
        gelu = sb("gelu", [128, 2, BU, T])
        band = sb("band", [128, 3 * W - 1, W])
        side = sb("side", [128, 2 * W * W])
        value = sb("value", [128, NWIN, HU * HS])
        stage = sb("stage", [128, 2, T])
        attn = sb("attn", [128, 2, T])
        comb = sb("comb", [128, HG, 128])
        comb_u = sb("comb_u", [128, 128])
        cproj_u = sb("cproj_u", [128, 128])
        blockW = sb("blockW", [HU * BD, 128])
        posb = sb("posb", [128, W])
        outw = sb("outw", [128, LQ, 32])
        half_db = sb("half_db", [128, 1])
        mask_sel = sb("mask_sel", [LQ, 128], BF16)
        mask_rows = sb("mask_rows", [LQ, PAD + T], BF16)
        stat = sb("stat", [128, 3, W])

        psum = ctx.enter_context(nc.psum_tensor("psum", [128, 8, 512], F32))
        self_ps = psum[:, 0:BU, :]
        logit_ps = psum[:, 4:6, :]
        turn_ps = psum[:, 6:8, :]

        damage = side[:, 0:W * W].rearrange("p (w i) -> p w i", w=W)
        bandT = side[:, :].rearrange("p (i r) -> p i r", r=128)
        wpart = band[:, W:2 * W, :]

        def col(name, rows=128):
            a, b = COL[name]
            return pack[0:rows, a:b]

        s_load = sem("inputs_loaded")
        s_setup_v = sem("setup_by_vector")
        s_setup_p = sem("setup_by_gpsimd")
        s_setup_t = sem("setup_by_tensor")

        areas = {
            "band": [band[:, :, :].rearrange("p a b -> p (a b)"), 0],
            "side": [side[:, :], 0],
            "diff": [diff[:, :, :, :].rearrange("p a b t -> p (a b t)"), 0],
            "gelu": [gelu[:, :, :, :].rearrange("p a b t -> p (a b t)"), 0],
            "table": [table[:, :, :].rearrange("p b t -> p (b t)"), 0],
        }

        def scratch(width, area):
            flat, at = areas[area]
            areas[area][1] = at + width
            return flat[:, at:at + width]

        norm_buffers = {
            "square": [scratch(T, "gelu") for _ in range(4)], "spread": [scratch(T, "gelu") for _ in range(4)],
            "diagonal": [scratch(T, "diff") for _ in range(4)], "small": [scratch(8, "diff") for _ in range(4)],
        }

        with nc.Block() as block:
            @block.sync
            def _(sp):
                sp.dma_start(pack[:, :], pack_dram).then_inc(s_load, 16)
                sp.dma_start(x[:, :, :], xT_dram).then_inc(s_load, 16)
                sp.wait_ge(s_load, 32)

            @block.gpsimd
            def _(pool):
                pool.memset(band[:, :, :], 0.0).then_inc(s_setup_p, 1)
                pool.memset(xn[:, :, 0:PAD], 0.0).then_inc(s_setup_p, 1)
                pool.memset(table[:, :, 0:PAD], 0.0).then_inc(s_setup_p, 1)
                pool.wait_ge(s_setup_p, 3)

            @block.vector
            def _(dve):
                dve.wait_ge(s_load, 32)
                dve.tensor_tensor(blockW[:, :], col("fusedT", HU * BD), col("headmask", HU * BD),
                                  ALU.mult).then_inc(s_setup_v, 1)
                dve.tensor_scalar(outw[:, :, :].rearrange("p l m -> p (l m)"), col("place"), col("out_w"), None,
                                  ALU.mult).then_inc(s_setup_v, 1)
                dve.tensor_scalar(half_db[:, :], col("damage_b"), 0.5, None, ALU.mult).then_inc(s_setup_v, 1)
                dve.tensor_copy(mask_sel[:, :], col("mask_place", LQ)).then_inc(s_setup_v, 1)
                dve.tensor_copy(mask_rows[:, :], col("mask_rows", LQ)).then_inc(s_setup_v, 1)
                dve.wait_ge(s_setup_t, 1)
                dve.tensor_copy(comb[:, :, :].rearrange("p g m -> p (g m)"), psum[:, 4, :]).then_inc(s_setup_v, 1)
                dve.tensor_scalar(posb[:, :], psum[:, 5, 0:W], col("strain_b"), None,
                                  ALU.add).then_inc(s_setup_v, 1)
                dve.wait_ge(s_setup_v, 7)

            @block.tensor
            def _(pe):
                pe.wait_ge(s_load, 32)
                pe.wait_ge(s_setup_v, 1)
                a = COL["disp"][0]
                for g in range(HG):
                    pe.matmul(psum[:, 4, g * 128:(g + 1) * 128], pack[0:HU * BD, a + g * 128:a + (g + 1) * 128],
                              blockW[:, :], start=True, stop=True)
                pe.matmul(psum[:, 5, 0:W], col("posT", BD), col("relT", BD),
                          start=True, stop=True).then_inc(s_setup_t, 1)

        common = dict(nc=nc, sem=sem, x=x, xn=xn, psum=psum, col=col, scratch=scratch, buffers=norm_buffers)
        first_norm(common)
        attention(nc, sem, dict(locals()))
        gates = FeedForwardBuffers(common)
        norm_and_gates(common, gates, "ffn1", gates.state)
        output_norm_and_mix(common, gates)
        norm_and_gates(common, gates, "ffn2", gates.state2, out_dram)


class Norm:

    def __init__(self, common, tag, x_bank, y_bank, depth, base=0):
        self.m, self.x_bank, self.y_bank = common, x_bank, y_bank
        self.set = lambda name, b: common["buffers"][name][base + b % depth]
        sem = common["sem"]
        self.centred = sem(tag + "_centred")
        self.squared = sem(tag + "_squared")
        self.summed = sem(tag + "_summed")
        self.guarded = sem(tag + "_guarded")
        self.rooted = sem(tag + "_rooted")
        self.diagonal = sem(tag + "_diagonal")
        self.spread = sem(tag + "_spread")
        self.fetched = sem(tag + "_fetched")
        self.scaled = sem(tag + "_scaled")

    def centre(self, pe, b):
        pe.matmul(self.x_bank(b), self.m["col"]("centre_w"), self.m["x"][:, b, :],
                  start=True, stop=True).then_inc(self.centred, 1)

    def square(self, act, b):
        act.wait_ge(self.centred, b + 1)
        act.activation(self.set("square", b), self.x_bank(b), ACT.Square).then_inc(self.squared, 1)

    def sums(self, pe, b):
        pe.wait_ge(self.squared, b + 1)
        for k in range(T // 128):
            mm = pe.matmul(self.y_bank(b)[:, k:k + 1], self.set("square", b)[:, k * 128:(k + 1) * 128],
                           self.m["col"]("mean_w")[:, 0:1], start=True, stop=True)
        mm.then_inc(self.summed, 1)

    def guard(self, dve, b):
        dve.wait_ge(self.summed, b + 1)
        dve.tensor_scalar(self.set("small", b)[:, 0:4], self.y_bank(b)[:, 0:4], EPS, None,
                          ALU.add).then_inc(self.guarded, 1)

    def root(self, pool, b):
        pool.wait_ge(self.guarded, b + 1)
        pool.tensor_tensor(self.set("small", b)[:, 4:8], self.set("small", b)[:, 0:4],
                           self.m["col"]("minus_half"), ALU.pow).then_inc(self.rooted, 1)

    def diag(self, dve, b):
        dve.wait_ge(self.rooted, b + 1)
        dve.tensor_tensor(self.set("diagonal", b).rearrange("p (k m) -> p k m", m=128),
                          self.m["col"]("ident").unsqueeze(1).broadcast_to([128, 4, 128]),
                          self.set("small", b)[:, 4:8].unsqueeze(2).broadcast_to([128, 4, 128]),
                          ALU.mult).then_inc(self.diagonal, 1)

    def spread_out(self, pe, b):
        pe.wait_ge(self.diagonal, b + 1)
        pe.matmul(self.y_bank(b), self.m["col"]("ones_w"), self.set("diagonal", b),
                  start=True, stop=True).then_inc(self.spread, 1)

    def fetch(self, act, b):
        act.wait_ge(self.spread, b + 1)
        act.copy(self.set("spread", b), self.y_bank(b)).then_inc(self.fetched, 1)

    def scale(self, dve, b):
        dve.wait_ge(self.fetched, b + 1)
        dve.tensor_tensor(self.m["xn"][:, b, PAD:], self.x_bank(b), self.set("spread", b),
                          ALU.mult).then_inc(self.scaled, 1)


def first_norm(m):
    nc, psum = m["nc"], m["psum"]
    norm = Norm(m, "norm1", lambda b: psum[:, b % 4, :], lambda b: psum[:, 4 + b % 4, :], 4)
    with nc.Block() as block:
        @block.tensor
        def _(pe):
            for t in range(B + 2):
                if t < B:
                    if t >= 4:
                        pe.wait_ge(norm.scaled, t - 3)
                    norm.centre(pe, t)
                if 0 <= t - 1 < B:
                    norm.sums(pe, t - 1)
                if 0 <= t - 2 < B:
                    norm.spread_out(pe, t - 2)

        @block.scalar
        def _(act):
            for t in range(B + 3):
                if t < B:
                    norm.square(act, t)
                if 0 <= t - 3 < B:
                    norm.fetch(act, t - 3)

        @block.gpsimd
        def _(pool):
            for b in range(B):
                norm.root(pool, b)

        @block.vector
        def _(dve):
            for t in range(1, B + 4):
                if 0 <= t - 4 < B:
                    norm.scale(dve, t - 4)
                if 0 <= t - 1 < B:
                    norm.guard(dve, t - 1)
                    norm.diag(dve, t - 1)
            dve.wait_ge(norm.scaled, B)


def attention(nc, sem, m):
    x, xn, table, diff, gelu, band, value = (m[k] for k in ("x", "xn", "table", "diff", "gelu", "band", "value"))
    stage, attn, comb, comb_u, cproj_u, posb, outw = (
        m[k] for k in ("stage", "attn", "comb", "comb_u", "cproj_u", "posb", "outw"))
    self_ps, logit_ps, turn_ps, damage, bandT, wpart, stat = (
        m[k] for k in ("self_ps", "logit_ps", "turn_ps", "damage", "bandT", "wpart", "stat"))
    mask_sel, mask_rows, half_db, col = m["mask_sel"], m["mask_rows"], m["half_db"], m["col"]
    logit_dram, value_dram, cp_dram = m["logit_dram"], m["value_dram"], m["cp_dram"]

    comb_ready = sem("comb_ready")
    self_ready = sem("self_ready")
    table_ready = sem("table_ready")
    diff_by_vector = sem("diff_by_vector")
    diff_by_gpsimd = sem("diff_by_gpsimd")
    gelu_done = sem("gelu_done")
    reduced = sem("reduced")
    staged = sem("staged")
    written = [sem("written_even"), sem("written_odd")]
    reread = sem("reread")
    tanh_done = sem("tanh_done")
    combined = sem("combined")
    maxed = sem("maxed")
    shifted = sem("shifted")
    exped = sem("exped")
    summed = sem("summed")
    recip_done = sem("recip_done")
    probs = sem("probs")
    turned = sem("turned")
    turned_out = sem("turned_out")
    weighted = sem("weighted")
    weighted_out = sem("weighted_out")
    projected = sem("projected")
    added = sem("added")
    unit_weights = sem("unit_weights")
    values_done = sem("values_done")
    values_out = sem("values_out")
    values_stored = [sem("values_stored_even"), sem("values_stored_odd")]

    ci = W // 4

    def chunk(t3, c):
        return t3[:, :, c * ci:(c + 1) * ci]

    vstage = m["side"][:, 0:1024].rearrange("p (k n) -> p k n", k=2)

    with nc.Block() as block:
        @block.tensor
        def _(pe):
            def unit(u, produce, consume, first=False):
                def turn(g):
                    pe.wait_ge(probs, 4 * (u - 1) + g // 4 + 1)
                    if g >= 2:
                        pe.wait_ge(turned_out, 16 * (u - 1) + g - 1)
                    for k in range(4):
                        i = 4 * g + k
                        mm = pe.transpose(turn_ps[:, g % 2, k * 128:(k + 1) * 128],
                                          band[:, W - 1 - i:3 * W - 1 - i, i], col("ident"))
                    mm.then_inc(turned, 1)

                def weigh(b):
                    pe.wait_ge(turned_out, 16 * u)
                    pe.wait_ge(unit_weights, 32 * u)
                    if b >= 2:
                        pe.wait_ge(added, 4 * (u - 1) + b - 1)
                    for tc in range(TC):
                        for h in range(HU):
                            r = (b * HU + h) * TC + tc
                            mm = pe.matmul(turn_ps[32 * h:32 * h + HS, b % 2, tc * W:(tc + 1) * W],
                                           value[:, b * TC + tc, h * HS:(h + 1) * HS],
                                           bandT[:, :, r], start=True, stop=True, tile_position=(0, 32 * h))
                    mm.then_inc(weighted, 1)

                def project(b):
                    pe.wait_ge(weighted_out, 4 * (u - 1) + b + 1)
                    pe.matmul(turn_ps[:, b % 2, :], cproj_u[:, :], attn[:, b % 2, :],
                              start=True, stop=True).then_inc(projected, 1)

                def values(g):
                    if g >= 2:
                        pe.wait_ge(values_out, g - 1)
                    for k in range(4):
                        b, tc = (4 * g + k) // TC, (4 * g + k) % TC
                        mm = pe.matmul(turn_ps[:, g % 2, k * 128:(k + 1) * 128],
                                       xn[:, b, tc * W:tc * W + 2 * W], col("valT"), start=True, stop=True)
                    mm.then_inc(values_done, 1)

                def own_columns(v, b):
                    pe.matmul(self_ps[:, b, :], comb_u[:, :],
                              xn[:, bass.ds((v // HG) % BG * BU + b, 1), PAD:].rearrange("p a t -> p (a t)"),
                              start=True, stop=True).then_inc(self_ready, 1)

                if first:
                    pe.wait_ge(comb_ready, 1)
                    for b in NEXT_ORDER:
                        own_columns(0, b)
                for s in range(SLOTS):
                    q, d, t0 = s // LQ, s % LQ, s // LQ * LQ
                    if produce:
                        pe.wait_ge(gelu_done, SLOTS * u + s + 1)
                        if d == 0:
                            if q >= 2 or not first:
                                pe.wait_ge(staged, NQ * u + q - 1)
                            pe.matmul(logit_ps[:, q % 2, :], mask_sel[:, :], mask_rows[:, PAD - t0:PAD - t0 + T],
                                      start=True, stop=False, skip_group_check=True)
                        for b in range(BU):
                            mm = pe.matmul(logit_ps[32 * b:32 * b + 32, q % 2, t0:], outw[:, d, :],
                                           gelu[:, s % 2, b, t0:], start=False, stop=(d == LQ - 1),
                                           tile_position=(0, 32 * b), skip_group_check=True)
                        mm.then_inc(reduced, 1)
                        if s == NEXT_G:
                            pe.wait_ge(comb_ready, u + 2)
                            pe.wait_ge(diff_by_vector, SLOTS * u + NEXT_G)
                        if NEXT_G <= s < NEXT_G + BU:
                            own_columns(u + 1, NEXT_ORDER[s - NEXT_G])
                    if first and s >= VALUES and (s - VALUES) % 3 == 0 and (s - VALUES) // 3 < 16:
                        values((s - VALUES) // 3)
                    if consume:
                        if TURN <= s < TURN + 16:
                            turn(s - TURN)
                        if s in WEIGH:
                            weigh(WEIGH.index(s))
                        if s in PROJECT:
                            project(PROJECT.index(s))

            unit(0, True, False, first=True)
            with pe.Fori(1, UNITS) as u:
                unit(u, True, True)
            unit(UNITS, False, True)

        @block.scalar
        def _(act):
            def unit(u, produce, consume, first=False):
                for s in range(SLOTS):
                    t0 = s // LQ * LQ
                    if consume and TANH <= s < TANH + 4:
                        c = s - TANH
                        act.wait_ge(reread, 16 * 2 * BU * u)
                        act.activation(chunk(damage, c), chunk(damage, c), ACT.Tanh, bias=half_db[:, :],
                                       scale=0.5).then_inc(tanh_done, 1)
                    if consume and s == EXPONENT:
                        for k in range(2):
                            act.wait_ge(shifted, 4 * (u - 1) + 2 * k + 2)
                            h = wpart[:, :, 2 * k * ci:2 * (k + 1) * ci]
                            act.activation(h, h, ACT.Exp).then_inc(exped, 1)
                    if produce:
                        act.wait_ge(diff_by_vector, SLOTS * u + s + 1)
                        act.wait_ge(diff_by_gpsimd, SLOTS * u + s + 1)
                        if s >= 2 or not first:
                            act.wait_ge(reduced, SLOTS * u + s - 1)
                        act.activation(gelu[:, s % 2, :, t0:], diff[:, s % ND, :, t0:], ACT.Gelu,
                                       bias=posb[:, s:s + 1]).then_inc(gelu_done, 1)

            unit(0, True, False, first=True)
            with act.Fori(1, UNITS) as u:
                unit(u, True, True)
            unit(UNITS, False, True)

        @block.vector
        def _(dve):
            def unit(u, produce, consume, first=False):
                def stage_quad(q):
                    dve.wait_ge(reduced, SLOTS * u + LQ * (q + 1))
                    if q >= 2 or not first:
                        dve.wait_ge(written[q % 2], 16 * LQ * (NQ // 2 * u + (q // 2 if q >= 0 else -1)))
                    dve.tensor_copy(stage[:, q % 2, :], logit_ps[:, q % 2, :]).then_inc(staged, 1)

                def softmax(s):
                    step = next((k for k in (COMBINE, MAXIMUM, SHIFT, TOTAL) if k <= s < k + 4), None)
                    if step is None:
                        return
                    c = s - step
                    v = chunk(wpart, c)
                    mx, sm, rc = (stat[:, k, c * ci:(c + 1) * ci] for k in range(3))
                    if step == COMBINE:
                        dve.wait_ge(tanh_done, 4 * (u - 1) + c + 1)
                        dve.scalar_tensor_tensor(v, chunk(damage, c), -5.0, v, ALU.mult,
                                                 ALU.add).then_inc(combined, 1)
                    if step == MAXIMUM:
                        dve.wait_ge(combined, 4 * (u - 1) + c + 1)
                        dve.tensor_reduce(mx, v.rearrange("p w i -> p i w"), AX_X, ALU.max).then_inc(maxed, 1)
                    if step == SHIFT:
                        dve.wait_ge(maxed, 4 * (u - 1) + c + 1)
                        dve.tensor_tensor(v, v, mx.unsqueeze(1).broadcast_to([128, W, ci]),
                                          ALU.subtract).then_inc(shifted, 1)
                    if step == TOTAL:
                        dve.wait_ge(exped, 2 * (u - 1) + c // 2 + 1)
                        dve.tensor_reduce(sm, v.rearrange("p w i -> p i w"), AX_X, ALU.add).then_inc(summed, 1)
                        dve.wait_ge(summed, 4 * (u - 1) + c + 1)
                        dve.reciprocal(rc, sm).then_inc(recip_done, 1)

                def turn_out(g):
                    dve.wait_ge(turned, 16 * (u - 1) + g + 1)
                    dve.tensor_copy(bandT[:, 4 * g:4 * g + 4, :].rearrange("p i r -> p (i r)"),
                                    turn_ps[:, g % 2, :]).then_inc(turned_out, 1)

                def weigh_out(b):
                    dve.wait_ge(weighted, 4 * (u - 1) + b + 1)
                    dve.tensor_copy(attn[:, b % 2, :], turn_ps[:, b % 2, :]).then_inc(weighted_out, 1)

                def add(b):
                    dve.wait_ge(projected, 4 * (u - 1) + b + 1)
                    xb = x[:, bass.ds(((u - 1) // HG) * BU + b, 1), :].rearrange("p a t -> p (a t)")
                    dve.tensor_tensor(xb, xb, turn_ps[:, b % 2, :], ALU.add).then_inc(added, 1)

                def values_out_(g):
                    dve.wait_ge(values_done, g + 1)
                    if g >= 2:
                        dve.wait_ge(values_stored[g % 2], 16 * HG * (g // 2))
                    dve.tensor_copy(vstage[:, g % 2, :], turn_ps[:, g % 2, :]).then_inc(values_out, 1)

                if produce:
                    if first:
                        dve.tensor_copy(comb_u[:, :], comb[:, 0, :]).then_inc(comb_ready, 1)
                    for n, b in enumerate(NEXT_ORDER):
                        dve.wait_ge(self_ready, 4 * u + n + 1)
                        if not first and n == 0:
                            dve.wait_ge(diff_by_gpsimd, SLOTS * u)
                            dve.wait_ge(diff_by_vector, SLOTS * u)
                        dve.tensor_copy(table[:, b, PAD:], self_ps[:, b, :]).then_inc(table_ready, 1)
                    dve.wait_ge(table_ready, 4 * u + 4)
                for s in range(SLOTS):
                    q, d, t0 = s // LQ, s % LQ, s // LQ * LQ
                    if produce:
                        nb = BU - POOL_BATCHES[s]
                        if s >= ND or not first:
                            dve.wait_ge(gelu_done, SLOTS * u + s - ND + 1)
                        own = self_ps[:, 0:nb, t0:] if s < NEXT_G else table[:, 0:nb, PAD + t0:]
                        dve.tensor_tensor(diff[:, s % ND, 0:nb, t0:], table[:, 0:nb, PAD + t0 - s:TP - s],
                                          own, ALU.subtract).then_inc(diff_by_vector, 1)
                        if d == 3 and q > 0:
                            stage_quad(q - 1)
                    if d == 3 and q == 0 and consume:
                        stage_quad(-1)
                    if first and s >= VALUES_OUT and (s - VALUES_OUT) % 3 == 0 and (s - VALUES_OUT) // 3 < 16:
                        values_out_((s - VALUES_OUT) // 3)
                    if produce and s == NEXT_G - ND:
                        dve.tensor_copy(comb_u[:, :], comb[:, bass.ds((u + 1) % HG, 1), :].rearrange(
                            "p a m -> p (a m)")).then_inc(comb_ready, 1)
                    if consume:
                        softmax(s)
                        if TURN_OUT <= s < TURN_OUT + 16:
                            turn_out(s - TURN_OUT)
                        if s in WEIGH_OUT:
                            weigh_out(WEIGH_OUT.index(s))
                        if s in ADD:
                            add(ADD.index(s))

            unit(0, True, False, first=True)
            with dve.Fori(1, UNITS) as u:
                unit(u, True, True)
            unit(UNITS, False, True)
            dve.wait_ge(added, 4 * UNITS)

        @block.gpsimd
        def _(pool):
            def unit(u, produce, consume, first=False):
                for s in range(SLOTS):
                    d, t0 = s % LQ, s // LQ * LQ
                    if produce:
                        nb = BU - POOL_BATCHES[s]
                        if s < 2:
                            pool.wait_ge(table_ready, 4 * u + (BU if s else POOL_BATCHES[0]))
                        if s >= ND or not first:
                            pool.wait_ge(gelu_done, SLOTS * u + s - ND + 1)
                        pool.tensor_tensor(diff[:, s % ND, nb:, t0:], table[:, nb:, PAD + t0 - s:TP - s],
                                           table[:, nb:, PAD + t0:], ALU.subtract).then_inc(diff_by_gpsimd, 1)
                    if consume and NORMALISE <= s < NORMALISE + 8 and (s - NORMALISE) % 2 == 0:
                        c = (s - NORMALISE) // 2
                        v = chunk(wpart, c)
                        pool.wait_ge(recip_done, 4 * (u - 1) + c + 1)
                        pool.tensor_tensor(v, v, stat[:, 2, c * ci:(c + 1) * ci].unsqueeze(1).broadcast_to(
                            [128, W, ci]), ALU.mult).then_inc(probs, 1)

            unit(0, True, False, first=True)
            with pool.Fori(1, UNITS) as u:
                unit(u, True, True)
            unit(UNITS, False, True)

        @block.sync
        def _(sp):
            def unit(u, produce, consume, first=False):
                def write(q):
                    sp.wait_ge(staged, NQ * u + q + 1)
                    v, qq = (u, q) if q >= 0 else (u - 1, NQ - 1)
                    for w in range(LQ):
                        dst = logit_dram[bass.ds(v, 1), :, :, W - LQ * (qq + 1) + w, :].rearrange(
                            "a r c i -> (a r) c i")
                        src = stage[w:128:LQ, q % 2, :].rearrange("r (c i) -> r c i", i=W)
                        sp.dma_start(dst, src).then_inc(written[q % 2], 16)

                def read():
                    sp.wait_ge(written[0], 16 * LQ * NQ // 2 * u)
                    sp.wait_ge(written[1], 16 * LQ * NQ // 2 * u)
                    for b in range(BU):
                        for kind, dst in ((0, wpart), (1, damage)):
                            r = (b * 2 + kind) * HU
                            src = logit_dram[bass.ds(u - 1, 1), r:r + HU, :, :, :].rearrange(
                                "a h c w i -> (a h c) w i")
                            sp.dma_start(dst[32 * b:32 * b + 32, :, :], src).then_inc(reread, 16)

                def weights():
                    sp.dma_start(cproj_u[:, :], cp_dram[bass.ds((u - 1) % HG, 1), :, :].rearrange(
                        "a p m -> (a p) m")).then_inc(unit_weights, 16)
                    sp.dma_start(value[:, :, :], value_dram[bass.ds(u - 1, 1), :, :, :].rearrange(
                        "a p n d -> (a p) n d")).then_inc(unit_weights, 16)

                def store_values(g):
                    sp.wait_ge(values_out, g + 1)
                    bg, n0 = (4 * g) // NWIN, (4 * g) % NWIN
                    for hg in range(HG):
                        src = vstage[:, g % 2, :].rearrange("p (k n) -> p k n", k=4)[:, :, hg * 32:(hg + 1) * 32]
                        sp.dma_start(value_dram[bg * HG + hg, :, n0:n0 + 4, :], src).then_inc(
                            values_stored[g % 2], 16)

                for q in range(NQ):
                    if q > 0:
                        if produce:
                            write(q - 1)
                    elif consume:
                        write(-1)
                        read()
                        weights()
                    if first:
                        for g in range(16):
                            if (3 * g + VALUES_OUT) // LQ == q:
                                store_values(g)
                if first:
                    for k in range(2):
                        sp.wait_ge(values_stored[k], 16 * HG * 8)

            unit(0, True, False, first=True)
            with sp.Fori(1, UNITS) as u:
                unit(u, True, True)
            unit(UNITS, False, True)
            for k in range(2):
                sp.wait_ge(written[k], 16 * LQ * NQ // 2 * UNITS)


class FeedForwardBuffers:

    def __init__(self, m):
        scratch = m["scratch"]
        self.rec = [scratch(C, "band") for _ in range(4)]
        self.bias = scratch(4, "band")
        self.ro = scratch(C, "band")
        self.state = [scratch(T, "band") for _ in range(2)]
        self.state2 = [scratch(T, "band") for _ in range(2)]
        self.gates = [scratch(T, "band") for _ in range(3)]
        self.prod = [scratch(T, "band") for _ in range(2)]
        self.out = [scratch(T, "band") for _ in range(2)]
        self.ready = m["sem"]("ffn_constants_ready")
        self.READY = 10

    def prepare(self, dve, col):
        for k, name in enumerate(("uf", "ui", "uc", "uo")):
            dve.tensor_scalar(self.rec[k], col(name), 0.5, None, ALU.mult).then_inc(self.ready, 1)
        dve.tensor_scalar(self.ro, col("ro"), 0.5, None, ALU.mult).then_inc(self.ready, 1)
        dve.tensor_scalar(self.bias[:, 0:1], col("bf"), 0.5, None, ALU.mult).then_inc(self.ready, 1)
        dve.tensor_scalar(self.bias[:, 1:2], col("bi"), 0.5, None, ALU.mult).then_inc(self.ready, 1)
        dve.tensor_copy(self.bias[:, 2:3], col("bc")).then_inc(self.ready, 1)
        for s in (self.state[0], self.state2[0]):
            dve.tensor_scalar(s, col("c0").broadcast_to([128, T]), 2.0, None, ALU.mult).then_inc(self.ready, 1)
        dve.wait_ge(self.ready, self.READY)


def norm_and_gates(m, ff, tag, state, out_dram=None):
    nc, sem, psum, x, xn, col = m["nc"], m["sem"], m["psum"], m["x"], m["xn"], m["col"]
    norm = Norm(m, tag + "_norm", lambda b: psum[:, 4 + b % 2, :], lambda b: psum[:, 6 + b % 2, :], 2)
    z = sem(tag + "_z")
    gated = sem(tag + "_gated")
    prods = sem(tag + "_products")
    stepped = sem(tag + "_stepped")
    out_z, out_tanh, out_added = sem(tag + "_out_z"), sem(tag + "_out_tanh"), sem(tag + "_out_added")
    stored = sem(tag + "_output_stored")
    HALF = T // 2
    AHEAD = 2
    zbank = [[psum[:, 2 * k, 0:HALF], psum[:, 2 * k, HALF:T], psum[:, 2 * k + 1, 0:HALF]] for k in range(2)]
    with nc.Block() as block:
        @block.tensor
        def _(pe):
            def centre(b):
                if b >= 2:
                    pe.wait_ge(norm.scaled, b - 1)
                norm.centre(pe, b)

            def inputs(b, k):
                pe.wait_ge(norm.scaled, b + 1)
                if b:
                    pe.wait_ge(gated, 6 * (b - 1) + 3 * k + 3)
                for g, name in enumerate(("wf", "wi", "wc")):
                    pe.matmul(zbank[k][g], col(name), xn[:, b, PAD + k * HALF:PAD + (k + 1) * HALF],
                              start=(g != 1), stop=False, skip_group_check=True)

            def recur(b, k):
                if b:
                    pe.wait_ge(stepped, 2 * (b - 1) + k + 1)
                for g in range(3):
                    mm = pe.matmul(zbank[k][g], ff.rec[g], state[b % 2][:, k * HALF:(k + 1) * HALF],
                                   start=False, stop=True, skip_group_check=True)
                    if g:
                        mm.then_inc(z, 1)

            for b in range(AHEAD):
                centre(b)
            for b in range(AHEAD):
                norm.sums(pe, b)
            for b in range(AHEAD):
                norm.spread_out(pe, b)
            pe.wait_ge(ff.ready, ff.READY)
            inputs(0, 0)
            inputs(0, 1)
            for b in range(B):
                more = b + AHEAD < B
                recur(b, 0)
                if more:
                    centre(b + AHEAD)
                recur(b, 1)
                if more:
                    norm.sums(pe, b + AHEAD)
                if b + 1 < B:
                    inputs(b + 1, 0)
                    inputs(b + 1, 1)
                if more:
                    norm.spread_out(pe, b + AHEAD)
            if out_dram is not None:
                for b in range(B):
                    if b >= 4:
                        pe.wait_ge(out_tanh, b - 3)
                    pe.matmul(psum[:, 4 + b % 4, :], col("wo"), xn[:, b, PAD:], start=True, stop=False)
                    if b == 0:
                        pe.wait_ge(stepped, 2 * B)
                    pe.matmul(psum[:, 4 + b % 4, :], ff.rec[3], state[B % 2], start=False,
                              stop=True).then_inc(out_z, 1)

        @block.scalar
        def _(act):
            for b in range(AHEAD):
                norm.square(act, b)
            for b in range(AHEAD):
                norm.fetch(act, b)
            for b in range(B):
                for k in range(2):
                    h = slice(k * HALF, (k + 1) * HALF)
                    for g in range(3):
                        act.wait_ge(z, 4 * b + 2 * k + (1 if g < 2 else 2))
                        if b and g == 0:
                            act.wait_ge(stepped, 2 * (b - 1) + k + 1)
                        act.activation(ff.gates[g][:, h], zbank[k][g], ACT.Tanh, bias=ff.bias[:, g:g + 1],
                                       scale=0.5 if g < 2 else 1.0).then_inc(gated, 1)
                    if b + AHEAD < B:
                        if k == 0:
                            norm.square(act, b + AHEAD)
                        else:
                            norm.fetch(act, b + AHEAD)
            if out_dram is not None:
                for b in range(B):
                    act.wait_ge(out_z, b + 1)
                    if b >= 2:
                        act.wait_ge(out_added, b - 1)
                    act.activation(ff.out[b % 2], psum[:, 4 + b % 4, :], ACT.Tanh,
                                   bias=col("bo")).then_inc(out_tanh, 1)

        @block.gpsimd
        def _(pool):
            for b in range(B):
                norm.root(pool, b)

        @block.vector
        def _(dve):
            if out_dram is None:
                ff.prepare(dve, col)
            for b in range(AHEAD):
                norm.guard(dve, b)
            for b in range(AHEAD):
                norm.diag(dve, b)
            for b in range(AHEAD):
                norm.scale(dve, b)
            for b in range(B):
                for k in range(2):
                    h = slice(k * HALF, (k + 1) * HALF)
                    dve.wait_ge(gated, 6 * b + 3 * k + 1)
                    dve.scalar_tensor_tensor(ff.prod[0][:, h], ff.gates[0][:, h], 1.0, state[b % 2][:, h],
                                             ALU.add, ALU.mult).then_inc(prods, 1)
                    dve.wait_ge(gated, 6 * b + 3 * k + 3)
                    dve.scalar_tensor_tensor(ff.prod[1][:, h], ff.gates[1][:, h], 1.0, ff.gates[2][:, h],
                                             ALU.add, ALU.mult).then_inc(prods, 1)
                    dve.wait_ge(prods, 4 * b + 2 * k + 2)
                    dve.scalar_tensor_tensor(state[(b + 1) % 2][:, h], ff.prod[0][:, h], 0.5,
                                             ff.prod[1][:, h], ALU.mult, ALU.add).then_inc(stepped, 1)
                    if b + AHEAD < B:
                        if k == 0:
                            norm.guard(dve, b + AHEAD)
                        else:
                            norm.diag(dve, b + AHEAD)
                            norm.scale(dve, b + AHEAD)
            if out_dram is None:
                dve.wait_ge(stepped, 2 * B)
            else:
                for b in range(B):
                    dve.wait_ge(out_tanh, b + 1)
                    dve.tensor_tensor(x[:, b, :], x[:, b, :], ff.out[b % 2], ALU.add).then_inc(out_added, 1)

        if out_dram is not None:
            @block.sync
            def _(sp):
                for b in range(B):
                    sp.wait_ge(out_added, b + 1)
                    sp.dma_start(out_dram[:, b, :], x[:, b, :]).then_inc(stored, 16)
                sp.wait_ge(stored, 16 * B)


def output_norm_and_mix(m, ff):
    nc, sem, psum, x, xn, col, scratch = (m[k] for k in ("nc", "sem", "psum", "x", "xn", "col", "scratch"))

    def two(area, width=T):
        return [scratch(width, area) for _ in range(2)]

    delta, v_sb, gate = two("side"), two("side"), two("side")
    mixed = [scratch(T, "side") for _ in range(3)]
    pp, aa, bb = two("side", T + 1), two("side", T + 1), two("side", T + 1)
    d1, d2 = scratch(T, "band"), scratch(T, "band")
    e1b, e2b, e1, e2 = two("band"), two("band"), two("band"), two("band")
    ev, part = scratch(T, "diff"), two("diff")
    den, num = two("diff"), two("diff")
    h_ps, x3, stats, k_ps, v_ps, r_ps, o_ps = (psum[:, k, :] for k in range(7))
    norm = Norm(m, "norm3", lambda b: x3, lambda b: stats, 2)

    init = sem("mix_buffers_initialised")
    hz, h_done, h_added = sem("h_z"), sem("h_tanh"), sem("h_added")
    delta_done = sem("mix_delta")
    mixed_done = sem("mix_mixed")
    k_done, v_done, r_done = sem("mix_k"), sem("mix_v"), sem("mix_r")
    v_copied, gate_done = sem("mix_v_copied"), sem("mix_gate_tanh")
    maximum = sem("mix_running_maximum")
    d1_done, d2_done = sem("mix_d1"), sem("mix_d2")
    args_b, args_r = sem("mix_carry_arguments"), sem("mix_read_arguments")
    exp_b, exp_r = sem("mix_carry_weights"), sem("mix_read_weights")
    ev_done, aa_done, bb_done = sem("mix_ev"), sem("mix_aa"), sem("mix_bb")
    part0_done, part1_done = sem("mix_e2_v"), sem("mix_e1_aa")
    num_done = sem("mix_numerator")
    den_done = sem("mix_denominator")
    inverted = sem("mix_denominator_inverted")
    ratio, gated = sem("mix_ratio"), sem("mix_gated")
    out_done, out_added = sem("mix_out"), sem("mix_out_added")

    def turns():
        for j in range(B + 4):
            yield tuple(j - age if 0 <= j - age < B else None for age in range(5))

    with nc.Block() as block:
        @block.tensor
        def _(pe):
            for b0, b1, b2, b3, b4 in turns():
                if b0 is not None:
                    b = b0
                    if b:
                        pe.wait_ge(h_done, b)
                    pe.matmul(h_ps, col("wo"), xn[:, b, PAD:], start=True, stop=False)
                    pe.matmul(h_ps, ff.rec[3], ff.state[B % 2], start=False, stop=True).then_inc(hz, 1)
                    pe.wait_ge(h_added, b + 1)
                    if b:
                        pe.wait_ge(norm.scaled, b)
                    norm.centre(pe, b)
                    norm.sums(pe, b)
                if b1 is not None:
                    b = b1
                    pe.wait_ge(mixed_done, 3 * b + 1)
                    if b:
                        pe.wait_ge(d2_done, b)
                    pe.matmul(k_ps, col("rk"), mixed[0], start=True, stop=True).then_inc(k_done, 1)
                    pe.wait_ge(mixed_done, 3 * b + 2)
                    if b:
                        pe.wait_ge(v_copied, b)
                    pe.matmul(v_ps, col("rv"), mixed[1], start=True, stop=True).then_inc(v_done, 1)
                if b0 is not None:
                    norm.spread_out(pe, b0)
                if b1 is not None:
                    b = b1
                    pe.wait_ge(mixed_done, 3 * b + 3)
                    if b:
                        pe.wait_ge(gate_done, b)
                    pe.matmul(r_ps, col("rr"), mixed[2], start=True, stop=True).then_inc(r_done, 1)
                if b3 is not None:
                    b = b3
                    pe.wait_ge(gated, b + 1)
                    if b:
                        pe.wait_ge(out_added, b)
                    pe.matmul(o_ps, ff.ro, gate[b % 2], start=True, stop=True).then_inc(out_done, 1)

        @block.scalar
        def _(act):
            for b0, b1, b2, b3, b4 in turns():
                if b2 is not None:
                    b, k = b2, b2 % 2
                    act.wait_ge(d2_done, b + 1)
                    if b >= 2:
                        act.wait_ge(part1_done, b - 1)
                        act.wait_ge(den_done, 2 * (b - 1))
                    act.activation(e1[k], d2, ACT.Relu).then_inc(args_r, 1)
                    act.activation(e2[k], d2, ACT.Relu, scale=-1.0).then_inc(args_r, 1)
                if b0 is not None:
                    b = b0
                    act.wait_ge(hz, b + 1)
                    if b >= 2:
                        act.wait_ge(h_added, b - 1)
                    act.activation(ff.out[b % 2], h_ps, ACT.Tanh, bias=col("bo")).then_inc(h_done, 1)
                if b2 is not None:
                    b, k = b2, b2 % 2
                    for n, t in enumerate((e1, e2)):
                        act.wait_ge(args_r, 2 * b + n + 1)
                        act.activation(t[k], t[k], ACT.Exp, scale=-1.0).then_inc(exp_r, 1)
                    act.wait_ge(r_done, b + 1)
                    if b >= 2:
                        act.wait_ge(out_done, b - 1)
                    act.activation(gate[k], r_ps, ACT.Tanh, scale=0.5).then_inc(gate_done, 1)
                if b0 is not None:
                    norm.square(act, b0)
                if b1 is not None:
                    b, k = b1, b1 % 2
                    act.wait_ge(v_done, b + 1)
                    if b >= 2:
                        act.wait_ge(part0_done, b - 1)
                    act.copy(v_sb[k], v_ps).then_inc(v_copied, 1)
                if b0 is not None:
                    norm.fetch(act, b0)
                if b1 is not None:
                    b, k = b1, b1 % 2
                    act.wait_ge(d1_done, b + 1)
                    if b >= 2:
                        act.wait_ge(aa_done, b - 1)
                    act.activation(e1b[k], d1, ACT.Relu, scale=-1.0).then_inc(args_b, 1)
                    act.activation(e2b[k], d1, ACT.Relu).then_inc(args_b, 1)
                    for n, t in enumerate((e1b, e2b)):
                        act.wait_ge(args_b, 2 * b + n + 1)
                        act.activation(t[k], t[k], ACT.Exp, scale=-1.0).then_inc(exp_b, 1)

        @block.gpsimd
        def _(pool):
            for k in range(2):
                pool.memset(pp[k][:, 0:1], NEG_INF).then_inc(init, 1)
                pool.memset(aa[k][:, 0:1], 0.0).then_inc(init, 1)
                pool.memset(bb[k][:, 0:1], 0.0).then_inc(init, 1)
            pool.wait_ge(init, 6)
            for b0, b1, b2, b3, b4 in turns():
                if b2 is not None:
                    b, k = b2, b2 % 2
                    pool.wait_ge(exp_b, 2 * b + 2)
                    pool.wait_ge(v_copied, b + 1)
                    if b:
                        pool.wait_ge(aa_done, b)
                    pool.tensor_tensor(ev, e2b[k], v_sb[k], ALU.mult).then_inc(ev_done, 1)
                if b0 is not None:
                    b = b0
                    pool.wait_ge(h_done, b + 1)
                    pool.tensor_tensor(x[:, b, :], x[:, b, :], ff.out[b % 2], ALU.add).then_inc(h_added, 1)
                if b2 is not None:
                    b, k = b2, b2 % 2
                    pool.wait_ge(exp_r, 2 * b + 2)
                    if b:
                        pool.wait_ge(num_done, b)
                    pool.tensor_tensor(part[0], e2[k], v_sb[k], ALU.mult).then_inc(part0_done, 1)
                    pool.wait_ge(aa_done, b + 1)
                    pool.tensor_tensor(part[1], e1[k], aa[k][:, 0:T], ALU.mult).then_inc(part1_done, 1)
                if b0 is not None:
                    norm.root(pool, b0)
                if b2 is not None:
                    b, k = b2, b2 % 2
                    pool.wait_ge(part0_done, b + 1)
                    pool.wait_ge(part1_done, b + 1)
                    if b >= 2:
                        pool.wait_ge(gated, b - 1)
                    pool.tensor_tensor(num[k], part[0], part[1], ALU.add).then_inc(num_done, 1)
                if b0 is not None:
                    b = b0
                    pool.wait_ge(norm.scaled, b + 1)
                    if b >= 2:
                        pool.wait_ge(mixed_done, 3 * (b - 1))
                    pool.tensor_tensor(delta[b % 2], xn[:, b, PAD:], xn[:, b, PAD - 1:TP - 1],
                                       ALU.subtract).then_inc(delta_done, 1)

        @block.vector
        def _(dve):
            dve.wait_ge(init, 6)
            for b0, b1, b2, b3, b4 in turns():
                if b3 is not None:
                    b, k = b3, b3 % 2
                    dve.wait_ge(num_done, b + 1)
                    dve.wait_ge(inverted, b + 1)
                    dve.tensor_tensor(num[k], num[k], den[k], ALU.mult).then_inc(ratio, 1)
                if b1 is not None:
                    b = b1
                    dve.wait_ge(delta_done, b + 1)
                    for n, (name, read) in enumerate((("mk", k_done), ("mv", v_done), ("mr", r_done))):
                        if b:
                            dve.wait_ge(read, b)
                        dve.scalar_tensor_tensor(mixed[n], delta[b % 2], col(name), xn[:, b, PAD - 1:TP - 1],
                                                 ALU.mult, ALU.add).then_inc(mixed_done, 1)
                if b2 is not None:
                    b, k = b2, b2 % 2
                    dve.wait_ge(exp_b, 2 * b + 2)
                    dve.tensor_tensor_scan(bb[k][:, 1:T + 1], e1b[k], e2b[k], 0.0, ALU.mult,
                                           ALU.add).then_inc(bb_done, 1)
                    dve.wait_ge(ev_done, b + 1)
                    if b >= 2:
                        dve.wait_ge(part1_done, b - 1)
                    dve.tensor_tensor_scan(aa[k][:, 1:T + 1], e1b[k], ev, 0.0, ALU.mult,
                                           ALU.add).then_inc(aa_done, 1)
                    dve.wait_ge(exp_r, 2 * b + 2)
                    dve.wait_ge(bb_done, b + 1)
                    dve.tensor_tensor(den[k], e1[k], bb[k][:, 0:T], ALU.mult).then_inc(den_done, 1)
                    dve.wait_ge(den_done, 2 * b + 1)
                    dve.scalar_tensor_tensor(den[k], e2[k], 1.0e-9, den[k], ALU.add, ALU.add).then_inc(den_done, 1)
                if b0 is not None:
                    norm.guard(dve, b0)
                if b2 is not None:
                    b, k = b2, b2 % 2
                    dve.wait_ge(den_done, 2 * b + 2)
                    dve.reciprocal(den[k], den[k]).then_inc(inverted, 1)
                if b3 is not None:
                    b, k = b3, b3 % 2
                    dve.wait_ge(ratio, b + 1)
                    dve.wait_ge(gate_done, b + 1)
                    dve.scalar_tensor_tensor(gate[k], gate[k], 1.0, num[k], ALU.add, ALU.mult).then_inc(gated, 1)
                if b4 is not None:
                    b = b4
                    dve.wait_ge(out_done, b + 1)
                    dve.tensor_tensor(x[:, b, :], x[:, b, :], o_ps, ALU.add).then_inc(out_added, 1)
                if b0 is not None:
                    norm.diag(dve, b0)
                if b1 is not None:
                    b, k = b1, b1 % 2
                    old, new = pp[k][:, 0:T], pp[k][:, 1:T + 1]
                    dve.wait_ge(k_done, b + 1)
                    dve.tensor_tensor_scan(new, col("td").broadcast_to([128, T]), k_ps, NEG_INF, ALU.add,
                                           ALU.max).then_inc(maximum, 1)
                    dve.wait_ge(maximum, b + 1)
                    if b:
                        dve.wait_ge(args_b, 2 * b)
                    dve.scalar_tensor_tensor(d1, old, col("td"), k_ps, ALU.add, ALU.subtract).then_inc(d1_done, 1)
                if b0 is not None:
                    norm.scale(dve, b0)
                if b1 is not None:
                    b, k = b1, b1 % 2
                    if b:
                        dve.wait_ge(args_r, 2 * b)
                    dve.scalar_tensor_tensor(d2, k_ps, col("tf"), pp[k][:, 0:T], ALU.add,
                                             ALU.subtract).then_inc(d2_done, 1)
            dve.wait_ge(out_added, B)


def kernel(**inputs):
    import numpy as np
    import concourse.bacc as bacc
    from concourse.bass_utils import run_bass_kernel_spmd as run

    A = {k: np.asarray(v) for k, v in inputs.items()}
    a = {k[len("L0_attn_a_"):]: v for k, v in A.items() if k.startswith("L0_attn_a_")}
    r = {k[len("L0_attn_b_"):]: v for k, v in A.items() if k.startswith("L0_attn_b_")}
    f = {k[len("L0_ffn_"):]: v for k, v in A.items() if k.startswith("L0_ffn_")}

    headmask = np.kron(np.eye(HU, dtype=np.float32), np.ones((BD, NF), np.float32))
    place = np.zeros((HU, 2, BD, LQ, 2, HU, LQ), np.float32)
    for h in range(HU):
        for kind in range(2):
            for lag in range(LQ):
                place[h, kind, :, lag, kind, h, LQ - 1 - lag] = 1.0
    mask_place = np.zeros((LQ, BU, 2, HU, LQ), np.float32)
    mask_rows = np.zeros((LQ, PAD + T), np.float32)
    for w in range(LQ):
        mask_place[w, :, 0, :, w] = 1.0
        mask_rows[w, :PAD + LQ - 1 - w] = MASKED

    def columns(v, n=1):
        return np.tile(np.asarray(v).reshape(-1, 1), (n, 1))

    parts = {
        "ident": np.eye(128, dtype=np.float32),
        "mean_w": np.full((128, 1), 1.0 / C, np.float32),
        "centre_w": np.eye(128, dtype=np.float32) - np.float32(1.0 / C),
        "ones_w": np.ones((128, 128), np.float32),
        "minus_half": np.full((128, 4), -0.5, np.float32),
        "headmask": headmask,
        "fusedT": np.tile(a["strain_fused_w"].T, (HU, HU)),
        "disp": a["W_disp"].reshape(HG, HU * BD, C).transpose(1, 0, 2).reshape(HU * BD, HG * C),
        "posT": np.tile(np.concatenate([a["pos_proj_w"].T, np.zeros((BD, BD), np.float32)], 1), (1, HU)),
        "relT": a["rel_pos_emb"][::-1].T,
        "place": place.reshape(128, LQ * 32),
        "valT": a["W_val"].T,
        "wf": f["wf"].T, "uf": f["uf"].T, "wi": f["wi"].T, "ui": f["ui"].T,
        "wc": f["wc"].T, "uc": f["uc"].T, "wo": f["wo"].T, "uo": f["uo"].T,
        "rk": r["W_k"].T, "rv": r["W_v"].T, "rr": r["W_r"].T, "ro": r["W_o"].T,
        "strain_b": columns(a["strain_fused_b"], HU),
        "out_w": columns(np.concatenate([a["bond_out_w"][0], a["damage_out_w"][0]]), HU),
        "damage_b": columns(a["damage_out_b"], 128),
        "bf": columns(f["bf"]), "bi": columns(f["bi"]), "bc": columns(f["bc"]), "bo": columns(f["bo"]),
        "c0": columns(f["in_c"]),
        "td": columns(r["time_decay"]), "tf": columns(r["time_first"]),
        "mk": columns(r["time_mix_k"]), "mv": columns(r["time_mix_v"]), "mr": columns(r["time_mix_r"]),
        "mask_place": mask_place.reshape(LQ, 128), "mask_rows": mask_rows,
    }
    pack = np.zeros((128, WIDTH), np.float32)
    for name, part in parts.items():
        lo, hi = COL[name]
        pack[:part.shape[0], lo:hi] = part
    cp = np.zeros((HG, HU, 32, C), np.float32)
    cp[:, :, :HS, :] = a["c_proj_w"].T.reshape(HG, HU, HS, C)
    xT = np.ascontiguousarray(a["x"].transpose(2, 0, 1))

    nc = bacc.Bacc("TRN2", target_bir_lowering=False, num_devices=1)
    arrays = {"xT": xT, "pack": pack, "cp": cp.reshape(HG, 128, C)}
    args = [nc.dram_tensor(k, v.shape, mybir.dt.from_np(v.dtype), kind="ExternalInput").ap()
            for k, v in arrays.items()]
    args.append(nc.dram_tensor("outT", (128, B, T), F32, kind="ExternalOutput").ap())
    program(nc, *args)
    res = run(nc, [arrays], core_ids=[0])
    return np.ascontiguousarray(res.results[0]["outT"].transpose(1, 2, 0))
```

```python
from contextlib import ExitStack

import concourse.bass as bass
from concourse import mybir

F32 = mybir.dt.float32
BF16 = mybir.dt.bfloat16
ALU = mybir.AluOpType
ACT = mybir.ActivationFunctionType
AX_X = mybir.AxisListType.X

C = 128
B, T = 8, 512
NH, HS, BD = 16, 8, 16
W = 64
HU, BU = 4, 4
NF = 2 * BD
HG, BG = NH // HU, B // BU
UNITS = HG * BG
LQ = 4
NQ = W // LQ
SLOTS = W
TC = T // W
ND = 6
PAD = W
TP = T + PAD
MASKED = -1.0e38
NEG_INF = -1.0e38
EPS = 1.0e-5

TANH, COMBINE, MAXIMUM, SHIFT = 12, 15, 19, 23
EXPONENT = 28
TOTAL, NORMALISE = 31, 32
TURN, TURN_OUT = 35, 38
WEIGH, WEIGH_OUT = (51, 53, 56, 58), (54, 56, 59, 61)
PROJECT, ADD = (54, 56, 59, 61), (57, 59, 62, 63)
CARRIED_ADD = (1, 2)
VALUES, VALUES_OUT = 3, 7
LATE = dict(centre=2, square=4, sums=4, guard=8, root=9, diag=10, spread=7, fetch=9, scale=13)
EARLY = 2
LATE_EVERY = 4
NEXT_G = 48
NEXT_ORDER = (3, 2, 1, 0)


def share_differences():
    shares, vector, gpsimd = [], 0.0, 0.0
    for s in range(SLOTS):
        vector += 1.8 * (COMBINE <= s < SHIFT + 4 or TOTAL <= s < TOTAL + 4)
        vector += (s % LQ == 3) + (TURN_OUT <= s < TURN_OUT + 16) + (s in ADD[:2]) + (s in CARRIED_ADD)
        gpsimd += 3.6 * (s in range(NORMALISE, NORMALISE + 8, 2))
        n = 2 if vector + (BU - 1) > gpsimd + 3.0 else 1
        vector, gpsimd = vector + BU - n, gpsimd + 2.05 * n
        shares.append(n)
    return shares


POOL_BATCHES = share_differences()


def user_before(s):
    return s - ND if s >= ND else max(t for t in range(SLOTS) if t % ND == s) - SLOTS

NWIN = BU * TC

_COLS = [
    ("ident", 128), ("mean_w", 1), ("centre_w", 128), ("ones_w", 128), ("minus_half", 4), ("headmask", 128), ("fusedT", 128), ("disp", HG * 128),
    ("posT", 128), ("relT", W), ("place", LQ * 32), ("valT", 128),
    ("wf", 128), ("uf", 128), ("wi", 128), ("ui", 128), ("wc", 128), ("uc", 128), ("wo", 128), ("uo", 128),
    ("rk", 128), ("rv", 128), ("rr", 128), ("ro", 128),
    ("strain_b", 1), ("out_w", 1), ("damage_b", 1),
    ("bf", 1), ("bi", 1), ("bc", 1), ("bo", 1), ("c0", 1),
    ("td", 1), ("tf", 1), ("mk", 1), ("mv", 1), ("mr", 1),
    ("mask_place", 128), ("mask_rows", PAD + T),
]
COL, WIDTH = {}, 0
for _name, _n in _COLS:
    COL[_name] = (WIDTH, WIDTH + _n)
    WIDTH += _n


def program(nc, xT_dram, pack_dram, cp_dram, out_dram):
    logit_dram = nc.dram_tensor("logit_scratch", (UNITS, BU * 2 * HU, TC, W, W), F32, kind="Internal").ap()
    value_dram = nc.dram_tensor("value_scratch", (UNITS, C, NWIN, HU * HS), F32, kind="Internal").ap()
    with ExitStack() as ctx:
        def sb(name, shape, dt=F32):
            return ctx.enter_context(nc.sbuf_tensor(name, shape, dt))

        def sem(name):
            return ctx.enter_context(nc.semaphore(name))

        x = sb("residual", [128, B, T])
        xn = sb("xn", [128, B, TP])
        pack = sb("weights", [128, WIDTH])
        table = sb("table", [128, BU, TP])
        diff = sb("diff", [128, ND, BU, T])
        band = sb("band", [128, 3 * W - 1, W])
        side = sb("side", [128, 2 * W * W])
        value = sb("value", [128, NWIN, HU * HS])
        stage = sb("stage", [128, 2, T])
        attn = sb("attn", [128, 2, T])
        comb = sb("comb", [128, HG, 128])
        comb_u = sb("comb_u", [128, 128])
        cproj_u = sb("cproj_u", [128, 128])
        blockW = sb("blockW", [HU * BD, 128])
        posb = sb("posb", [128, W])
        outw = sb("outw", [128, LQ, 32])
        half_db = sb("half_db", [128, 1])
        mask_sel = sb("mask_sel", [LQ, 128], BF16)
        mask_rows = sb("mask_rows", [LQ, PAD + T], BF16)
        stat = sb("stat", [128, 3, W])

        psum = ctx.enter_context(nc.psum_tensor("psum", [128, 8, 512], F32))
        self_ps = psum[:, 0:BU, :]
        logit_ps = psum[:, 4:6, :]
        turn_ps = psum[:, 6:8, :]

        damage = side[:, 0:W * W].rearrange("p (w i) -> p w i", w=W)
        bandT = side[:, :].rearrange("p (i r) -> p i r", r=128)
        wpart = band[:, W:2 * W, :]

        def col(name, rows=128):
            a, b = COL[name]
            return pack[0:rows, a:b]

        s_load = sem("weights_loaded")
        s_x = [sem("x_loaded_%d" % b) for b in range(BU)]
        s_x_late = sem("late_x_loaded")
        s_setup_v = sem("setup_by_vector")
        s_setup_p = sem("setup_by_gpsimd")
        s_setup_t = sem("setup_by_tensor")

        areas = {
            "band": [band[:, :, :].rearrange("p a b -> p (a b)"), 0],
            "side": [side[:, :], 0],
            "diff": [diff[:, :, :, :].rearrange("p a b t -> p (a b t)"), 0],
            "table": [table[:, :, :].rearrange("p b t -> p (b t)"), 0],
        }

        def scratch(width, area):
            flat, at = areas[area]
            areas[area][1] = at + width
            return flat[:, at:at + width]

        norm_buffers = {
            "square": [scratch(T, "diff") for _ in range(4)], "spread": [scratch(T, "diff") for _ in range(4)],
            "diagonal": [scratch(T, "diff") for _ in range(4)], "small": [scratch(8, "diff") for _ in range(4)],
        }

        common = dict(nc=nc, sem=sem, x=x, xn=xn, psum=psum, col=col, scratch=scratch, buffers=norm_buffers)
        late_norm_buffers = {name: [side[:, at + k * width:at + (k + 1) * width] for k in range(2)]
                             for name, at, width in (("square", 1024, T), ("spread", 1024 + 2 * T, T),
                                                     ("diagonal", 1024 + 4 * T, T), ("small", 1024 + 6 * T, 8))}
        norm = Norm(common, "norm1", lambda b: psum[:, b, :], lambda b: psum[:, 4 + b, :], BU)

        with nc.Block() as block:
            @block.sync
            def _(sp):
                sp.dma_start(pack[:, :], pack_dram).then_inc(s_load, 16)
                for b in range(BU):
                    sp.dma_start(x[:, b, :], xT_dram[:, b, :]).then_inc(s_x[b], 16)
                sp.dma_start(x[:, BU:, :], xT_dram[:, BU:, :]).then_inc(s_x_late, 16)

            @block.gpsimd
            def _(pool):
                pool.memset(xn[:, :, 0:PAD], 0.0).then_inc(s_setup_p, 1)
                pool.memset(table[:, :, 0:PAD], 0.0).then_inc(s_setup_p, 1)
                pool.memset(band[:, :, :], 0.0).then_inc(s_setup_p, 1)
                pool.wait_ge(s_setup_p, 3)
                for b in range(BU):
                    norm.root(pool, b)

            @block.scalar
            def _(act):
                for b in range(BU):
                    norm.square(act, b)
                for b in range(BU):
                    norm.fetch(act, b)

            @block.vector
            def _(dve):
                dve.wait_ge(s_load, 16)
                dve.tensor_tensor(blockW[:, :], col("fusedT", HU * BD), col("headmask", HU * BD),
                                  ALU.mult).then_inc(s_setup_v, 1)
                dve.tensor_scalar(outw[:, :, :].rearrange("p l m -> p (l m)"), col("place"), col("out_w"), None,
                                  ALU.mult).then_inc(s_setup_v, 1)
                dve.tensor_scalar(half_db[:, :], col("damage_b"), 0.5, None, ALU.mult).then_inc(s_setup_v, 1)
                dve.tensor_copy(mask_sel[:, :], col("mask_place", LQ)).then_inc(s_setup_v, 1)
                dve.tensor_copy(mask_rows[:, :], col("mask_rows", LQ)).then_inc(s_setup_v, 1)
                dve.wait_ge(s_setup_t, 1)
                dve.tensor_copy(comb[:, :, :].rearrange("p g m -> p (g m)"), psum[:, 6, :]).then_inc(s_setup_v, 1)
                dve.tensor_scalar(posb[:, :], psum[:, 7, 0:W], col("strain_b"), None,
                                  ALU.add).then_inc(s_setup_v, 1)
                norm.guard(dve, 0)
                norm.guard(dve, 1)
                norm.diag(dve, 0)
                norm.guard(dve, 2)
                norm.diag(dve, 1)
                norm.guard(dve, 3)
                norm.diag(dve, 2)
                norm.scale(dve, 0)
                norm.diag(dve, 3)
                for b in range(1, BU):
                    norm.scale(dve, b)
                dve.wait_ge(s_setup_v, 7)
                dve.wait_ge(norm.scaled, BU)

            @block.tensor
            def _(pe):
                pe.wait_ge(s_load, 16)
                pe.wait_ge(s_setup_v, 1)
                a = COL["disp"][0]
                for g in range(HG):
                    pe.matmul(psum[:, 6, g * 128:(g + 1) * 128], pack[0:HU * BD, a + g * 128:a + (g + 1) * 128],
                              blockW[:, :], start=True, stop=True)
                pe.matmul(psum[:, 7, 0:W], col("posT", BD), col("relT", BD),
                          start=True, stop=True).then_inc(s_setup_t, 1)
                for b in range(BU):
                    pe.wait_ge(s_x[b], 16)
                    norm.centre(pe, b)
                for b in range(BU):
                    if b == 2:
                        pe.wait_ge(s_setup_v, 7)
                    norm.sums(pe, b)
                for b in range(BU):
                    norm.spread_out(pe, b)

        ff = FeedForwardBuffers(common)
        gate_pass = GatePass(common, ff, "ffn1", ff.state)
        attention(nc, sem, dict(locals()))
        first_gates(common, gate_pass)
        output_norm_and_mix(common, ff)
        second_pass(common, ff, out_dram)


class Norm:

    def __init__(self, common, tag, x_bank, y_bank, depth, start=0):
        self.m, self.x_bank, self.y_bank, self.start = common, x_bank, y_bank, start
        self.set = lambda name, b: common["buffers"][name][b % depth]
        sem = common["sem"]
        self.centred = sem(tag + "_centred")
        self.squared = sem(tag + "_squared")
        self.summed = sem(tag + "_summed")
        self.guarded = sem(tag + "_guarded")
        self.rooted = sem(tag + "_rooted")
        self.diagonal = sem(tag + "_diagonal")
        self.spread = sem(tag + "_spread")
        self.fetched = sem(tag + "_fetched")
        self.scaled = sem(tag + "_scaled")

    def centre(self, pe, b):
        pe.matmul(self.x_bank(b), self.m["col"]("centre_w"), self.m["x"][:, b, :],
                  start=True, stop=True).then_inc(self.centred, 1)

    def square(self, act, b):
        act.wait_ge(self.centred, b + 1 - self.start)
        act.activation(self.set("square", b), self.x_bank(b), ACT.Square).then_inc(self.squared, 1)

    def sums(self, pe, b):
        pe.wait_ge(self.squared, b + 1 - self.start)
        for k in range(T // 128):
            mm = pe.matmul(self.y_bank(b)[:, k:k + 1], self.set("square", b)[:, k * 128:(k + 1) * 128],
                           self.m["col"]("mean_w")[:, 0:1], start=True, stop=True)
        mm.then_inc(self.summed, 1)

    def guard(self, dve, b):
        dve.wait_ge(self.summed, b + 1 - self.start)
        dve.tensor_scalar(self.set("small", b)[:, 0:4], self.y_bank(b)[:, 0:4], EPS, None,
                          ALU.add).then_inc(self.guarded, 1)

    def root(self, pool, b):
        pool.wait_ge(self.guarded, b + 1 - self.start)
        pool.tensor_tensor(self.set("small", b)[:, 4:8], self.set("small", b)[:, 0:4],
                           self.m["col"]("minus_half"), ALU.pow).then_inc(self.rooted, 1)

    def diag(self, dve, b):
        dve.wait_ge(self.rooted, b + 1 - self.start)
        dve.tensor_tensor(self.set("diagonal", b).rearrange("p (k m) -> p k m", m=128),
                          self.m["col"]("ident").unsqueeze(1).broadcast_to([128, 4, 128]),
                          self.set("small", b)[:, 4:8].unsqueeze(2).broadcast_to([128, 4, 128]),
                          ALU.mult).then_inc(self.diagonal, 1)

    def spread_out(self, pe, b):
        pe.wait_ge(self.diagonal, b + 1 - self.start)
        pe.matmul(self.y_bank(b), self.m["col"]("ones_w"), self.set("diagonal", b),
                  start=True, stop=True).then_inc(self.spread, 1)

    def fetch(self, act, b):
        act.wait_ge(self.spread, b + 1 - self.start)
        act.copy(self.set("spread", b), self.y_bank(b)).then_inc(self.fetched, 1)

    def scale(self, dve, b):
        dve.wait_ge(self.fetched, b + 1 - self.start)
        dve.tensor_tensor(self.m["xn"][:, b, PAD:], self.x_bank(b), self.set("spread", b),
                          ALU.mult).then_inc(self.scaled, 1)


def attention(nc, sem, m):
    x, xn, table, diff, band, value = (m[k] for k in ("x", "xn", "table", "diff", "band", "value"))
    stage, attn, comb, comb_u, cproj_u, posb, outw = (
        m[k] for k in ("stage", "attn", "comb", "comb_u", "cproj_u", "posb", "outw"))
    self_ps, logit_ps, turn_ps, damage, bandT, wpart, stat = (
        m[k] for k in ("self_ps", "logit_ps", "turn_ps", "damage", "bandT", "wpart", "stat"))
    s_x_late, gate_pass = m["s_x_late"], m["gate_pass"]
    mask_sel, mask_rows, half_db, col = m["mask_sel"], m["mask_rows"], m["half_db"], m["col"]
    logit_dram, value_dram, cp_dram = m["logit_dram"], m["value_dram"], m["cp_dram"]

    comb_ready = sem("comb_ready")
    self_ready = sem("self_ready")
    table_ready = sem("table_ready")
    diff_by_vector = sem("diff_by_vector")
    diff_by_gpsimd = sem("diff_by_gpsimd")
    gelu_done = sem("gelu_done")
    reduced = sem("reduced")
    staged = sem("staged")
    written = [sem("written_even"), sem("written_odd")]
    damage_reread = sem("damage_reread")
    bond_reread = sem("bond_reread")
    tanh_done = sem("tanh_done")
    combined = sem("combined")
    maxed = sem("maxed")
    shifted = sem("shifted")
    exped = sem("exped")
    summed = sem("summed")
    recip_done = sem("recip_done")
    probs = sem("probs")
    turned = sem("turned")
    turned_out = sem("turned_out")
    weighted = sem("weighted")
    weighted_out = sem("weighted_out")
    projected = sem("projected")
    added = sem("added")
    unit_weights = sem("unit_weights")
    values_done = sem("values_done")
    values_out = sem("values_out")
    values_stored = [sem("values_stored_even"), sem("values_stored_odd")]

    ci = W // 4

    def chunk(t3, c):
        return t3[:, :, c * ci:(c + 1) * ci]

    late = Norm(dict(m["common"], buffers=m["late_norm_buffers"]), "late_norm1",
                lambda b: m["psum"][:, b % 2, :], lambda b: m["psum"][:, 2 + b % 2, :], 2, start=BU)

    def late_batch(s, step):
        i = s - LATE[step]
        return BU + i // LATE_EVERY if i >= 0 and i % LATE_EVERY == 0 and i // LATE_EVERY < B - BU else None

    vstage = m["side"][:, 0:1024].rearrange("p (k n) -> p k n", k=2)

    with nc.Block() as block:
        @block.tensor
        def _(pe):
            def unit(u, produce, consume, first=False):
                def turn(g):
                    pe.wait_ge(probs, 4 * (u - 1) + g // 4 + 1)
                    if g >= 2:
                        pe.wait_ge(turned_out, 16 * (u - 1) + g - 1)
                    for k in range(4):
                        i = 4 * g + k
                        mm = pe.transpose(turn_ps[:, g % 2, k * 128:(k + 1) * 128],
                                          band[:, W - 1 - i:3 * W - 1 - i, i], col("ident"))
                    mm.then_inc(turned, 1)

                def weigh(b):
                    pe.wait_ge(turned_out, 16 * u)
                    pe.wait_ge(unit_weights, 32 * u)
                    if b >= 2:
                        pe.wait_ge(added, 4 * (u - 1) + b - 1)
                    for tc in range(TC):
                        for h in range(HU):
                            r = (b * HU + h) * TC + tc
                            mm = pe.matmul(turn_ps[32 * h:32 * h + HS, b % 2, tc * W:(tc + 1) * W],
                                           value[:, b * TC + tc, h * HS:(h + 1) * HS],
                                           bandT[:, :, r], start=True, stop=True, tile_position=(0, 32 * h))
                    mm.then_inc(weighted, 1)

                def project(b):
                    pe.wait_ge(weighted_out, 4 * (u - 1) + b + 1)
                    pe.matmul(turn_ps[:, b % 2, :], cproj_u[:, :], attn[:, b % 2, :],
                              start=True, stop=True).then_inc(projected, 1)

                def values(g):
                    if g >= 2:
                        pe.wait_ge(values_out, g - 1)
                    if 4 * g // TC >= BU:
                        pe.wait_ge(late.scaled, 4 * g // TC - BU + 1)
                    for k in range(4):
                        b, tc = (4 * g + k) // TC, (4 * g + k) % TC
                        mm = pe.matmul(turn_ps[:, g % 2, k * 128:(k + 1) * 128],
                                       xn[:, b, tc * W:tc * W + 2 * W], col("valT"), start=True, stop=True)
                    mm.then_inc(values_done, 1)

                def own_columns(v, b):
                    pe.matmul(self_ps[:, b, :], comb_u[:, :],
                              xn[:, bass.ds((v // HG) % BG * BU + b, 1), PAD:].rearrange("p a t -> p (a t)"),
                              start=True, stop=True).then_inc(self_ready, 1)

                if first:
                    pe.wait_ge(comb_ready, 1)
                    for b in range(BU):
                        own_columns(0, b)
                for s in range(SLOTS):
                    q, d, t0 = s // LQ, s % LQ, s // LQ * LQ
                    if produce:
                        pe.wait_ge(gelu_done, SLOTS * u + s + 1)
                        if d == 0:
                            if q >= 2 or not first:
                                pe.wait_ge(staged, NQ * u + q - 1)
                            pe.matmul(logit_ps[:, q % 2, :], mask_sel[:, :], mask_rows[:, PAD - t0:PAD - t0 + T],
                                      start=True, stop=False, skip_group_check=True)
                        for b in range(BU):
                            mm = pe.matmul(logit_ps[32 * b:32 * b + 32, q % 2, t0:], outw[:, d, :],
                                           diff[:, s % ND, b, t0:], start=False, stop=(d == LQ - 1),
                                           tile_position=(0, 32 * b), skip_group_check=True)
                        mm.then_inc(reduced, 1)
                        if s == NEXT_G:
                            pe.wait_ge(comb_ready, u + 2)
                            pe.wait_ge(diff_by_vector, SLOTS * u + NEXT_G)
                        if NEXT_G <= s < NEXT_G + BU:
                            own_columns(u + 1, NEXT_ORDER[s - NEXT_G])
                    if first:
                        if (b := late_batch(s, "centre")) is not None:
                            if b == BU:
                                pe.wait_ge(s_x_late, 16)
                                pe.wait_ge(table_ready, BU)
                            elif b >= BU + 2:
                                pe.wait_ge(late.scaled, b - BU - 1)
                            late.centre(pe, b)
                        if (b := late_batch(s, "sums")) is not None:
                            late.sums(pe, b)
                        if (b := late_batch(s, "spread")) is not None:
                            late.spread_out(pe, b)
                    if first and s >= VALUES and (s - VALUES) % 3 == 0 and (s - VALUES) // 3 < 16:
                        values((s - VALUES) // 3)
                    if consume:
                        if TURN <= s < TURN + 16:
                            turn(s - TURN)
                        if s in WEIGH:
                            weigh(WEIGH.index(s))
                        if s in PROJECT:
                            project(PROJECT.index(s))

            unit(0, True, False, first=True)
            with pe.Fori(1, UNITS) as u:
                unit(u, True, True)
            pe.wait_ge(staged, NQ * UNITS)
            gate_pass.open_tensor(pe)
            for b in range(EARLY):
                gate_pass.turn_tensor(pe, b)
            unit(UNITS, False, True)

        @block.scalar
        def _(act):
            def unit(u, produce, consume, first=False):
                for s in range(SLOTS):
                    t0 = s // LQ * LQ
                    if consume and TANH <= s < TANH + 4:
                        c = s - TANH
                        act.wait_ge(damage_reread, 16 * BU * u)
                        act.activation(chunk(damage, c), chunk(damage, c), ACT.Tanh, bias=half_db[:, :],
                                       scale=0.5).then_inc(tanh_done, 1)
                    if consume and s == EXPONENT:
                        for k in range(2):
                            act.wait_ge(shifted, 4 * (u - 1) + 2 * k + 2)
                            h = wpart[:, :, 2 * k * ci:2 * (k + 1) * ci]
                            act.activation(h, h, ACT.Exp).then_inc(exped, 1)
                    if consume and s in WEIGH_OUT:
                        b = WEIGH_OUT.index(s)
                        act.wait_ge(weighted, 4 * (u - 1) + b + 1)
                        act.copy(attn[:, b % 2, :], turn_ps[:, b % 2, :]).then_inc(weighted_out, 1)
                    if first:
                        if (b := late_batch(s, "square")) is not None:
                            late.square(act, b)
                        if (b := late_batch(s, "fetch")) is not None:
                            late.fetch(act, b)
                    if produce:
                        act.wait_ge(diff_by_vector, SLOTS * u + s + 1)
                        act.wait_ge(diff_by_gpsimd, SLOTS * u + s + 1)
                        v = diff[:, s % ND, :, t0:]
                        act.activation(v, v, ACT.Gelu,
                                       bias=posb[:, s:s + 1]).then_inc(gelu_done, 1)

            unit(0, True, False, first=True)
            with act.Fori(1, UNITS) as u:
                unit(u, True, True)
            gate_pass.open_scalar(act)
            for b in range(EARLY):
                gate_pass.turn_scalar(act, b)
            unit(UNITS, False, True)

        @block.vector
        def _(dve):
            def unit(u, produce, consume, first=False, carried=True):
                def stage_quad(q):
                    dve.wait_ge(reduced, SLOTS * u + LQ * (q + 1))
                    if q >= 2 or not first:
                        dve.wait_ge(written[q % 2], 16 * LQ * (NQ // 2 * u + (q // 2 if q >= 0 else -1)))
                    dve.tensor_copy(stage[:, q % 2, :], logit_ps[:, q % 2, :]).then_inc(staged, 1)

                def softmax(s):
                    step = next((k for k in (COMBINE, MAXIMUM, SHIFT, TOTAL) if k <= s < k + 4), None)
                    if step is None:
                        return
                    c = s - step
                    v = chunk(wpart, c)
                    mx, sm, rc = (stat[:, k, c * ci:(c + 1) * ci] for k in range(3))
                    if step == COMBINE:
                        dve.wait_ge(tanh_done, 4 * (u - 1) + c + 1)
                        dve.wait_ge(bond_reread, 16 * BU * u)
                        dve.scalar_tensor_tensor(v, chunk(damage, c), -5.0, v, ALU.mult,
                                                 ALU.add).then_inc(combined, 1)
                    if step == MAXIMUM:
                        dve.wait_ge(combined, 4 * (u - 1) + c + 1)
                        dve.tensor_reduce(mx, v.rearrange("p w i -> p i w"), AX_X, ALU.max).then_inc(maxed, 1)
                    if step == SHIFT:
                        dve.wait_ge(maxed, 4 * (u - 1) + c + 1)
                        dve.tensor_tensor(v, v, mx.unsqueeze(1).broadcast_to([128, W, ci]),
                                          ALU.subtract).then_inc(shifted, 1)
                    if step == TOTAL:
                        dve.wait_ge(exped, 2 * (u - 1) + c // 2 + 1)
                        dve.tensor_reduce(sm, v.rearrange("p w i -> p i w"), AX_X, ALU.add).then_inc(summed, 1)
                        dve.wait_ge(summed, 4 * (u - 1) + c + 1)
                        dve.reciprocal(rc, sm).then_inc(recip_done, 1)

                def turn_out(g):
                    dve.wait_ge(turned, 16 * (u - 1) + g + 1)
                    dve.tensor_copy(bandT[:, 4 * g:4 * g + 4, :].rearrange("p i r -> p (i r)"),
                                    turn_ps[:, g % 2, :]).then_inc(turned_out, 1)

                def add(b, v=u):
                    dve.wait_ge(projected, 4 * (v - 1) + b + 1)
                    xb = x[:, bass.ds(((v - 1) // HG) * BU + b, 1), :].rearrange("p a t -> p (a t)")
                    dve.tensor_tensor(xb, xb, turn_ps[:, b % 2, :], ALU.add).then_inc(added, 1)

                def values_out_(g):
                    dve.wait_ge(values_done, g + 1)
                    if g >= 2:
                        dve.wait_ge(values_stored[g % 2], 16 * HG * (g // 2))
                    dve.tensor_copy(vstage[:, g % 2, :], turn_ps[:, g % 2, :]).then_inc(values_out, 1)

                def fill_table(v, first_unit=False):
                    if not first_unit:
                        dve.wait_ge(diff_by_gpsimd, SLOTS * v)
                        dve.wait_ge(diff_by_vector, SLOTS * v)
                    for n, b in enumerate(range(BU) if first_unit else NEXT_ORDER):
                        dve.wait_ge(self_ready, 4 * v + n + 1)
                        dve.tensor_copy(table[:, b, PAD:], self_ps[:, b, :]).then_inc(table_ready, 1)

                if first:
                    dve.tensor_copy(comb_u[:, :], comb[:, 0, :]).then_inc(comb_ready, 1)
                    fill_table(0, first_unit=True)
                if produce:
                    dve.wait_ge(table_ready, 4 * u + 4)
                for s in range(SLOTS):
                    q, d, t0 = s // LQ, s % LQ, s // LQ * LQ
                    if produce:
                        nb = BU - POOL_BATCHES[s]
                        if s >= ND or not first:
                            dve.wait_ge(reduced, SLOTS * u + user_before(s) + 1)
                        own = self_ps[:, 0:nb, t0:] if s < NEXT_G and not first else table[:, 0:nb, PAD + t0:]
                        dve.tensor_tensor(diff[:, s % ND, 0:nb, t0:], table[:, 0:nb, PAD + t0 - s:TP - s],
                                          own, ALU.subtract).then_inc(diff_by_vector, 1)
                        if s == SLOTS - 1:
                            fill_table(u + 1)
                        if d == 3 and q > 0:
                            stage_quad(q - 1)
                    if carried and s in CARRIED_ADD:
                        add(2 + CARRIED_ADD.index(s), u - 1)
                    if d == 3 and q == 0 and consume:
                        stage_quad(-1)
                    if consume and not produce and s == LQ:
                        gate_pass.ff.prepare(dve, col)
                        gate_pass.open_vector(dve)
                        for b in range(EARLY):
                            gate_pass.turn_vector(dve, b)
                    if first:
                        if (b := late_batch(s, "guard")) is not None:
                            late.guard(dve, b)
                        if (b := late_batch(s, "diag")) is not None:
                            late.diag(dve, b)
                        if (b := late_batch(s, "scale")) is not None:
                            late.scale(dve, b)
                    if first and s >= VALUES_OUT and (s - VALUES_OUT) % 3 == 0 and (s - VALUES_OUT) // 3 < 16:
                        values_out_((s - VALUES_OUT) // 3)
                    if produce and s == NEXT_G - 4:
                        dve.tensor_copy(comb_u[:, :], comb[:, bass.ds((u + 1) % HG, 1), :].rearrange(
                            "p a m -> p (a m)")).then_inc(comb_ready, 1)
                    if consume:
                        softmax(s)
                        if TURN_OUT <= s < TURN_OUT + 16:
                            turn_out(s - TURN_OUT)
                        if s in ADD and (ADD.index(s) < 2 or not produce):
                            add(ADD.index(s))

            unit(0, True, False, first=True, carried=False)
            unit(1, True, True, carried=False)
            with dve.Fori(2, UNITS) as u:
                unit(u, True, True)
            unit(UNITS, False, True)
            dve.wait_ge(added, 4 * UNITS)

        @block.gpsimd
        def _(pool):
            def unit(u, produce, consume, first=False):
                for s in range(SLOTS):
                    d, t0 = s % LQ, s // LQ * LQ
                    if produce:
                        nb = BU - POOL_BATCHES[s]
                        if s < 2:
                            pool.wait_ge(table_ready, 4 * u + (BU if s or first else POOL_BATCHES[0]))
                        if s >= ND or not first:
                            pool.wait_ge(reduced, SLOTS * u + user_before(s) + 1)
                        pool.tensor_tensor(diff[:, s % ND, nb:, t0:], table[:, nb:, PAD + t0 - s:TP - s],
                                           table[:, nb:, PAD + t0:], ALU.subtract).then_inc(diff_by_gpsimd, 1)
                    if first and (b := late_batch(s, "root")) is not None:
                        late.root(pool, b)
                    if consume and NORMALISE <= s < NORMALISE + 8 and (s - NORMALISE) % 2 == 0:
                        c = (s - NORMALISE) // 2
                        v = chunk(wpart, c)
                        pool.wait_ge(recip_done, 4 * (u - 1) + c + 1)
                        pool.tensor_tensor(v, v, stat[:, 2, c * ci:(c + 1) * ci].unsqueeze(1).broadcast_to(
                            [128, W, ci]), ALU.mult).then_inc(probs, 1)

            unit(0, True, False, first=True)
            with pool.Fori(1, UNITS) as u:
                unit(u, True, True)
            for b in range(EARLY + GatePass.AHEAD):
                gate_pass.norm.root(pool, b)
            unit(UNITS, False, True)

        @block.sync
        def _(sp):
            def unit(u, produce, consume, first=False):
                def write(q):
                    sp.wait_ge(staged, NQ * u + q + 1)
                    v, qq = (u, q) if q >= 0 else (u - 1, NQ - 1)
                    for w in range(LQ):
                        dst = logit_dram[bass.ds(v, 1), :, :, W - LQ * (qq + 1) + w, :].rearrange(
                            "a r c i -> (a r) c i")
                        src = stage[w:128:LQ, q % 2, :].rearrange("r (c i) -> r c i", i=W)
                        sp.dma_start(dst, src).then_inc(written[q % 2], 16)

                def read():
                    sp.wait_ge(written[0], 16 * LQ * NQ // 2 * u)
                    sp.wait_ge(written[1], 16 * LQ * NQ // 2 * u)
                    for kind, dst, back in ((1, damage, damage_reread), (0, wpart, bond_reread)):
                        for b in range(BU):
                            r = (b * 2 + kind) * HU
                            src = logit_dram[bass.ds(u - 1, 1), r:r + HU, :, :, :].rearrange(
                                "a h c w i -> (a h c) w i")
                            sp.dma_start(dst[32 * b:32 * b + 32, :, :], src).then_inc(back, 16)

                def weights():
                    sp.dma_start(cproj_u[:, :], cp_dram[bass.ds((u - 1) % HG, 1), :, :].rearrange(
                        "a p m -> (a p) m")).then_inc(unit_weights, 16)
                    sp.dma_start(value[:, :, :], value_dram[bass.ds(u - 1, 1), :, :, :].rearrange(
                        "a p n d -> (a p) n d")).then_inc(unit_weights, 16)

                def store_values(g):
                    sp.wait_ge(values_out, g + 1)
                    bg, n0 = (4 * g) // NWIN, (4 * g) % NWIN
                    for hg in range(HG):
                        src = vstage[:, g % 2, :].rearrange("p (k n) -> p k n", k=4)[:, :, hg * 32:(hg + 1) * 32]
                        sp.dma_start(value_dram[bg * HG + hg, :, n0:n0 + 4, :], src).then_inc(
                            values_stored[g % 2], 16)

                for q in range(NQ):
                    if q > 0:
                        if produce:
                            write(q - 1)
                    elif consume:
                        write(-1)
                        read()
                        weights()
                    if first:
                        for g in range(16):
                            if (3 * g + VALUES_OUT) // LQ == q:
                                store_values(g)
                if first:
                    for k in range(2):
                        sp.wait_ge(values_stored[k], 16 * HG * 8)

            unit(0, True, False, first=True)
            with sp.Fori(1, UNITS) as u:
                unit(u, True, True)
            unit(UNITS, False, True)
            for k in range(2):
                sp.wait_ge(written[k], 16 * LQ * NQ // 2 * UNITS)


class FeedForwardBuffers:

    def __init__(self, m):
        scratch = m["scratch"]
        self.rec = [scratch(C, "diff") for _ in range(4)]
        self.bias = scratch(4, "diff")
        self.ro = scratch(C, "diff")
        self.state = [scratch(T, "diff") for _ in range(2)]
        self.state2 = [scratch(T, "diff") for _ in range(2)]
        self.gates = [scratch(T, "diff") for _ in range(3)]
        self.prod = [scratch(T, "diff") for _ in range(2)]
        self.out = [scratch(T, "table") for _ in range(2)]
        self.ready = m["sem"]("ffn_constants_ready")
        self.READY = 10

    def prepare(self, dve, col):
        for k, name in enumerate(("uf", "ui", "uc", "uo")):
            dve.tensor_scalar(self.rec[k], col(name), 0.5, None, ALU.mult).then_inc(self.ready, 1)
        dve.tensor_scalar(self.ro, col("ro"), 0.5, None, ALU.mult).then_inc(self.ready, 1)
        dve.tensor_scalar(self.bias[:, 0:1], col("bf"), 0.5, None, ALU.mult).then_inc(self.ready, 1)
        dve.tensor_scalar(self.bias[:, 1:2], col("bi"), 0.5, None, ALU.mult).then_inc(self.ready, 1)
        dve.tensor_copy(self.bias[:, 2:3], col("bc")).then_inc(self.ready, 1)
        for s in (self.state[0], self.state2[0]):
            dve.tensor_scalar(s, col("c0").broadcast_to([128, T]), 2.0, None, ALU.mult).then_inc(self.ready, 1)
        dve.wait_ge(self.ready, self.READY)


class GatePass:
    AHEAD = 2
    HALF = T // 2

    def __init__(self, m, ff, tag, state):
        sem, psum = m["sem"], m["psum"]
        self.m, self.ff, self.state = m, ff, state
        self.norm = Norm(m, tag + "_norm", lambda b: psum[:, 4 + b % 2, :], lambda b: psum[:, 6 + b % 2, :], 2)
        self.z = sem(tag + "_z")
        self.gated = sem(tag + "_gated")
        self.prods = sem(tag + "_products")
        self.stepped = sem(tag + "_stepped")
        self.zbank = [[psum[:, 2 * k, 0:self.HALF], psum[:, 2 * k, self.HALF:T],
                       psum[:, 2 * k + 1, 0:self.HALF]] for k in range(2)]

    def half(self, k):
        return slice(k * self.HALF, (k + 1) * self.HALF)

    def centre(self, pe, b):
        if b >= 2:
            pe.wait_ge(self.norm.scaled, b - 1)
        self.norm.centre(pe, b)

    def inputs(self, pe, b, k):
        pe.wait_ge(self.norm.scaled, b + 1)
        if b:
            pe.wait_ge(self.gated, 6 * (b - 1) + 3 * k + 3)
        for g, name in enumerate(("wf", "wi", "wc")):
            pe.matmul(self.zbank[k][g], self.m["col"](name),
                      self.m["xn"][:, b, PAD + k * self.HALF:PAD + (k + 1) * self.HALF],
                      start=(g != 1), stop=False, skip_group_check=True)

    def recur(self, pe, b, k):
        if b:
            pe.wait_ge(self.stepped, 2 * (b - 1) + k + 1)
        for g in range(3):
            mm = pe.matmul(self.zbank[k][g], self.ff.rec[g], self.state[b % 2][:, self.half(k)],
                           start=False, stop=True, skip_group_check=True)
            if g:
                mm.then_inc(self.z, 1)

    def open_tensor(self, pe):
        for b in range(self.AHEAD):
            self.centre(pe, b)
        for b in range(self.AHEAD):
            self.norm.sums(pe, b)
        for b in range(self.AHEAD):
            self.norm.spread_out(pe, b)
        pe.wait_ge(self.ff.ready, self.ff.READY)
        self.inputs(pe, 0, 0)
        self.inputs(pe, 0, 1)

    def turn_tensor(self, pe, b):
        ahead = b + self.AHEAD
        self.recur(pe, b, 0)
        if ahead < B:
            self.centre(pe, ahead)
        self.recur(pe, b, 1)
        if ahead < B:
            self.norm.sums(pe, ahead)
        if b + 1 < B:
            self.inputs(pe, b + 1, 0)
            self.inputs(pe, b + 1, 1)
        if ahead < B:
            self.norm.spread_out(pe, ahead)

    def open_scalar(self, act):
        for b in range(self.AHEAD):
            self.norm.square(act, b)
        for b in range(self.AHEAD):
            self.norm.fetch(act, b)

    def turn_scalar(self, act, b):
        ahead = b + self.AHEAD
        for k in range(2):
            for g in range(3):
                act.wait_ge(self.z, 4 * b + 2 * k + (1 if g < 2 else 2))
                if b and g == 0:
                    act.wait_ge(self.stepped, 2 * (b - 1) + k + 1)
                act.activation(self.ff.gates[g][:, self.half(k)], self.zbank[k][g], ACT.Tanh,
                               bias=self.ff.bias[:, g:g + 1],
                               scale=0.5 if g < 2 else 1.0).then_inc(self.gated, 1)
            if ahead < B:
                if k == 0:
                    self.norm.square(act, ahead)
                else:
                    self.norm.fetch(act, ahead)

    def open_vector(self, dve):
        for b in range(self.AHEAD):
            self.norm.guard(dve, b)
        for b in range(self.AHEAD):
            self.norm.diag(dve, b)
        for b in range(self.AHEAD):
            self.norm.scale(dve, b)

    def turn_vector(self, dve, b):
        ff, state, ahead = self.ff, self.state, b + self.AHEAD
        for k in range(2):
            h = self.half(k)
            dve.wait_ge(self.gated, 6 * b + 3 * k + 1)
            dve.scalar_tensor_tensor(ff.prod[0][:, h], ff.gates[0][:, h], 1.0, state[b % 2][:, h],
                                     ALU.add, ALU.mult).then_inc(self.prods, 1)
            dve.wait_ge(self.gated, 6 * b + 3 * k + 3)
            dve.scalar_tensor_tensor(ff.prod[1][:, h], ff.gates[1][:, h], 1.0, ff.gates[2][:, h],
                                     ALU.add, ALU.mult).then_inc(self.prods, 1)
            dve.wait_ge(self.prods, 4 * b + 2 * k + 2)
            dve.scalar_tensor_tensor(state[(b + 1) % 2][:, h], ff.prod[0][:, h], 0.5,
                                     ff.prod[1][:, h], ALU.mult, ALU.add).then_inc(self.stepped, 1)
            if ahead < B:
                if k == 0:
                    self.norm.guard(dve, ahead)
                else:
                    self.norm.diag(dve, ahead)
                    self.norm.scale(dve, ahead)


def first_gates(m, gate_pass):
    with m["nc"].Block() as block:
        @block.tensor
        def _(pe):
            for b in range(EARLY, B):
                gate_pass.turn_tensor(pe, b)

        @block.scalar
        def _(act):
            for b in range(EARLY, B):
                gate_pass.turn_scalar(act, b)

        @block.gpsimd
        def _(pool):
            for b in range(EARLY + GatePass.AHEAD, B):
                gate_pass.norm.root(pool, b)

        @block.vector
        def _(dve):
            for b in range(EARLY, B):
                gate_pass.turn_vector(dve, b)
            dve.wait_ge(gate_pass.stepped, 2 * B)


def second_pass(m, ff, out_dram):
    nc, sem, psum, x, xn, col = m["nc"], m["sem"], m["psum"], m["x"], m["xn"], m["col"]
    gate_pass = GatePass(m, ff, "ffn2", ff.state2)
    out_z, out_tanh, out_added = sem("ffn2_out_z"), sem("ffn2_out_tanh"), sem("ffn2_out_added")
    stored = sem("output_stored")
    with nc.Block() as block:
        @block.tensor
        def _(pe):
            gate_pass.open_tensor(pe)
            for b in range(B):
                gate_pass.turn_tensor(pe, b)
            for b in range(B):
                if b >= 4:
                    pe.wait_ge(out_tanh, b - 3)
                pe.matmul(psum[:, 4 + b % 4, :], col("wo"), xn[:, b, PAD:], start=True, stop=False)
                if b == 0:
                    pe.wait_ge(gate_pass.stepped, 2 * B)
                pe.matmul(psum[:, 4 + b % 4, :], ff.rec[3], ff.state2[B % 2], start=False,
                          stop=True).then_inc(out_z, 1)

        @block.scalar
        def _(act):
            gate_pass.open_scalar(act)
            for b in range(B):
                gate_pass.turn_scalar(act, b)
            for b in range(B):
                act.wait_ge(out_z, b + 1)
                if b >= 2:
                    act.wait_ge(out_added, b - 1)
                act.activation(ff.out[b % 2], psum[:, 4 + b % 4, :], ACT.Tanh,
                               bias=col("bo")).then_inc(out_tanh, 1)

        @block.gpsimd
        def _(pool):
            for b in range(B):
                gate_pass.norm.root(pool, b)

        @block.vector
        def _(dve):
            gate_pass.open_vector(dve)
            for b in range(B):
                gate_pass.turn_vector(dve, b)
            for b in range(B):
                dve.wait_ge(out_tanh, b + 1)
                dve.tensor_tensor(x[:, b, :], x[:, b, :], ff.out[b % 2], ALU.add).then_inc(out_added, 1)

        @block.sync
        def _(sp):
            for b in range(B):
                sp.wait_ge(out_added, b + 1)
                sp.dma_start(out_dram[:, b, :], x[:, b, :]).then_inc(stored, 16)
            sp.wait_ge(stored, 16 * B)


def output_norm_and_mix(m, ff):
    nc, sem, psum, x, xn, col, scratch = (m[k] for k in ("nc", "sem", "psum", "x", "xn", "col", "scratch"))

    def two(area, width=T):
        return [scratch(width, area) for _ in range(2)]

    delta, v_sb, gate = two("side"), two("side"), two("side")
    mixed = [scratch(T, "side") for _ in range(3)]
    pp, aa, bb = two("side", T + 1), two("side", T + 1), two("side", T + 1)
    d1, d2 = scratch(T, "band"), scratch(T, "band")
    e1b, e2b, e1, e2 = two("band"), two("band"), two("band"), two("band")
    ev, part = scratch(T, "band"), two("band")
    den, num = two("band"), two("band")
    h_ps, x3, stats, k_ps, v_ps, r_ps, o_ps = (psum[:, k, :] for k in range(7))
    norm = Norm(m, "norm3", lambda b: x3, lambda b: stats, 2)

    init = sem("mix_buffers_initialised")
    hz, h_done, h_added = sem("h_z"), sem("h_tanh"), sem("h_added")
    delta_done = sem("mix_delta")
    mixed_done = sem("mix_mixed")
    k_done, v_done, r_done = sem("mix_k"), sem("mix_v"), sem("mix_r")
    v_copied, gate_done = sem("mix_v_copied"), sem("mix_gate_tanh")
    maximum = sem("mix_running_maximum")
    d1_done, d2_done = sem("mix_d1"), sem("mix_d2")
    args_b, args_r = sem("mix_carry_arguments"), sem("mix_read_arguments")
    exp_b, exp_r = sem("mix_carry_weights"), sem("mix_read_weights")
    ev_done, aa_done, bb_done = sem("mix_ev"), sem("mix_aa"), sem("mix_bb")
    part0_done, part1_done = sem("mix_e2_v"), sem("mix_e1_aa")
    num_done = sem("mix_numerator")
    den_done = sem("mix_denominator")
    inverted = sem("mix_denominator_inverted")
    ratio, gated = sem("mix_ratio"), sem("mix_gated")
    out_done, out_added = sem("mix_out"), sem("mix_out_added")

    def turns():
        for j in range(B + 5):
            yield tuple(j - age if 0 <= j - age < B else None for age in range(6))

    with nc.Block() as block:
        @block.tensor
        def _(pe):
            for b0, b1, b2, b3, b4, b5 in turns():
                if b0 is not None:
                    b = b0
                    if b:
                        pe.wait_ge(h_done, b)
                    pe.matmul(h_ps, col("wo"), xn[:, b, PAD:], start=True, stop=False)
                    pe.matmul(h_ps, ff.rec[3], ff.state[B % 2], start=False, stop=True).then_inc(hz, 1)
                if b1 is not None:
                    b = b1
                    pe.wait_ge(h_added, b + 1)
                    if b:
                        pe.wait_ge(norm.scaled, b)
                    norm.centre(pe, b)
                    norm.sums(pe, b)
                if b2 is not None:
                    b = b2
                    pe.wait_ge(mixed_done, 3 * b + 2)
                    if b:
                        pe.wait_ge(v_copied, b)
                    pe.matmul(v_ps, col("rv"), mixed[1], start=True, stop=True).then_inc(v_done, 1)
                    if b:
                        pe.wait_ge(d1_done, b)
                    pe.matmul(k_ps, col("rk"), mixed[0], start=True, stop=True).then_inc(k_done, 1)
                if b1 is not None:
                    norm.spread_out(pe, b1)
                if b2 is not None:
                    b = b2
                    pe.wait_ge(mixed_done, 3 * b + 3)
                    if b:
                        pe.wait_ge(gate_done, b)
                    pe.matmul(r_ps, col("rr"), mixed[2], start=True, stop=True).then_inc(r_done, 1)
                if b4 is not None:
                    b = b4
                    pe.wait_ge(gated, b + 1)
                    if b:
                        pe.wait_ge(out_added, b)
                    pe.matmul(o_ps, ff.ro, gate[b % 2], start=True, stop=True).then_inc(out_done, 1)

        @block.scalar
        def _(act):
            for b0, b1, b2, b3, b4, b5 in turns():
                if b3 is not None:
                    b, k = b3, b3 % 2
                    act.wait_ge(d2_done, b + 1)
                    if b >= 2:
                        act.wait_ge(part1_done, b - 1)
                        act.wait_ge(den_done, 2 * (b - 1))
                    act.activation(e1[k], d2, ACT.Relu).then_inc(args_r, 1)
                    act.activation(e2[k], d2, ACT.Relu, scale=-1.0).then_inc(args_r, 1)
                    for n, t in enumerate((e1, e2)):
                        act.wait_ge(args_r, 2 * b + n + 1)
                        act.activation(t[k], t[k], ACT.Exp, scale=-1.0).then_inc(exp_r, 1)
                if b0 is not None:
                    b = b0
                    act.wait_ge(hz, b + 1)
                    if b >= 2:
                        act.wait_ge(h_added, b - 1)
                    act.activation(ff.out[b % 2], h_ps, ACT.Tanh, bias=col("bo")).then_inc(h_done, 1)
                if b1 is not None:
                    norm.square(act, b1)
                if b3 is not None:
                    b, k = b3, b3 % 2
                    act.wait_ge(r_done, b + 1)
                    if b >= 2:
                        act.wait_ge(out_done, b - 1)
                    act.activation(gate[k], r_ps, ACT.Tanh, scale=0.5).then_inc(gate_done, 1)
                if b2 is not None:
                    b, k = b2, b2 % 2
                    act.wait_ge(v_done, b + 1)
                    if b >= 2:
                        act.wait_ge(part0_done, b - 1)
                    act.copy(v_sb[k], v_ps).then_inc(v_copied, 1)
                if b1 is not None:
                    norm.fetch(act, b1)
                if b2 is not None:
                    b, k = b2, b2 % 2
                    act.wait_ge(d1_done, b + 1)
                    if b >= 2:
                        act.wait_ge(aa_done, b - 1)
                    act.activation(e1b[k], d1, ACT.Relu, scale=-1.0).then_inc(args_b, 1)
                    act.activation(e2b[k], d1, ACT.Relu).then_inc(args_b, 1)
                    for n, t in enumerate((e1b, e2b)):
                        act.wait_ge(args_b, 2 * b + n + 1)
                        act.activation(t[k], t[k], ACT.Exp, scale=-1.0).then_inc(exp_b, 1)

        @block.gpsimd
        def _(pool):
            for k in range(2):
                pool.memset(pp[k][:, 0:1], NEG_INF).then_inc(init, 1)
                pool.memset(aa[k][:, 0:1], 0.0).then_inc(init, 1)
                pool.memset(bb[k][:, 0:1], 0.0).then_inc(init, 1)
            pool.wait_ge(init, 6)
            for b0, b1, b2, b3, b4, b5 in turns():
                if b0 is not None:
                    b = b0
                    pool.wait_ge(h_done, b + 1)
                    pool.tensor_tensor(x[:, b, :], x[:, b, :], ff.out[b % 2], ALU.add).then_inc(h_added, 1)
                if b3 is not None:
                    b, k = b3, b3 % 2
                    pool.wait_ge(exp_b, 2 * b + 2)
                    pool.wait_ge(v_copied, b + 1)
                    if b:
                        pool.wait_ge(aa_done, b)
                    pool.tensor_tensor(ev, e2b[k], v_sb[k], ALU.mult).then_inc(ev_done, 1)
                if b1 is not None:
                    norm.root(pool, b1)
                if b3 is not None:
                    b, k = b3, b3 % 2
                    pool.wait_ge(exp_r, 2 * b + 2)
                    if b:
                        pool.wait_ge(num_done, b)
                    pool.tensor_tensor(part[0], e2[k], v_sb[k], ALU.mult).then_inc(part0_done, 1)
                if b1 is not None:
                    b = b1
                    pool.wait_ge(norm.scaled, b + 1)
                    if b >= 2:
                        pool.wait_ge(mixed_done, 3 * (b - 1))
                    pool.tensor_tensor(delta[b % 2], xn[:, b, PAD:], xn[:, b, PAD - 1:TP - 1],
                                       ALU.subtract).then_inc(delta_done, 1)
                if b3 is not None:
                    b, k = b3, b3 % 2
                    pool.wait_ge(aa_done, b + 1)
                    pool.tensor_tensor(part[1], e1[k], aa[k][:, 0:T], ALU.mult).then_inc(part1_done, 1)
                    pool.wait_ge(part0_done, b + 1)
                    pool.wait_ge(part1_done, b + 1)
                    if b >= 2:
                        pool.wait_ge(gated, b - 1)
                    pool.tensor_tensor(num[k], part[0], part[1], ALU.add).then_inc(num_done, 1)

        @block.vector
        def _(dve):
            def mix(b, n):
                if b:
                    dve.wait_ge((k_done, v_done, r_done)[n], b)
                dve.scalar_tensor_tensor(mixed[n], delta[b % 2], col(("mk", "mv", "mr")[n]),
                                         xn[:, b, PAD - 1:TP - 1], ALU.mult, ALU.add).then_inc(mixed_done, 1)

            dve.wait_ge(init, 6)
            for b0, b1, b2, b3, b4, b5 in turns():
                if b2 is not None:
                    dve.wait_ge(delta_done, b2 + 1)
                    mix(b2, 0)
                    mix(b2, 1)
                if b3 is not None:
                    b, k = b3, b3 % 2
                    dve.wait_ge(exp_b, 2 * b + 2)
                    dve.tensor_tensor_scan(bb[k][:, 1:T + 1], e1b[k], e2b[k], 0.0, ALU.mult,
                                           ALU.add).then_inc(bb_done, 1)
                if b5 is not None:
                    b = b5
                    dve.wait_ge(out_done, b + 1)
                    dve.tensor_tensor(x[:, b, :], x[:, b, :], o_ps, ALU.add).then_inc(out_added, 1)
                if b1 is not None:
                    norm.guard(dve, b1)
                if b3 is not None:
                    b, k = b3, b3 % 2
                    dve.wait_ge(exp_r, 2 * b + 2)
                    dve.wait_ge(bb_done, b + 1)
                    dve.tensor_tensor(den[k], e1[k], bb[k][:, 0:T], ALU.mult).then_inc(den_done, 1)
                if b2 is not None:
                    mix(b2, 2)
                if b4 is not None:
                    b, k = b4, b4 % 2
                    dve.wait_ge(num_done, b + 1)
                    dve.wait_ge(inverted, b + 1)
                    dve.tensor_tensor(num[k], num[k], den[k], ALU.mult).then_inc(ratio, 1)
                if b1 is not None:
                    norm.diag(dve, b1)
                if b4 is not None:
                    b, k = b4, b4 % 2
                    dve.wait_ge(ratio, b + 1)
                    dve.wait_ge(gate_done, b + 1)
                    dve.scalar_tensor_tensor(gate[k], gate[k], 1.0, num[k], ALU.add, ALU.mult).then_inc(gated, 1)
                if b3 is not None:
                    b, k = b3, b3 % 2
                    dve.wait_ge(den_done, 2 * b + 1)
                    dve.scalar_tensor_tensor(den[k], e2[k], 1.0e-9, den[k], ALU.add, ALU.add).then_inc(den_done, 1)
                if b2 is not None:
                    b, k = b2, b2 % 2
                    old, new = pp[k][:, 0:T], pp[k][:, 1:T + 1]
                    dve.wait_ge(k_done, b + 1)
                    dve.tensor_tensor_scan(new, col("td").broadcast_to([128, T]), k_ps, NEG_INF, ALU.add,
                                           ALU.max).then_inc(maximum, 1)
                    dve.wait_ge(maximum, b + 1)
                    if b:
                        dve.wait_ge(args_r, 2 * b)
                    dve.scalar_tensor_tensor(d2, k_ps, col("tf"), old, ALU.add, ALU.subtract).then_inc(d2_done, 1)
                    if b:
                        dve.wait_ge(args_b, 2 * b)
                    dve.scalar_tensor_tensor(d1, old, col("td"), k_ps, ALU.add, ALU.subtract).then_inc(d1_done, 1)
                if b1 is not None:
                    norm.scale(dve, b1)
                if b3 is not None:
                    b, k = b3, b3 % 2
                    dve.wait_ge(ev_done, b + 1)
                    if b >= 2:
                        dve.wait_ge(part1_done, b - 1)
                    dve.tensor_tensor_scan(aa[k][:, 1:T + 1], e1b[k], ev, 0.0, ALU.mult,
                                           ALU.add).then_inc(aa_done, 1)
                    dve.wait_ge(den_done, 2 * b + 2)
                    dve.reciprocal(den[k], den[k]).then_inc(inverted, 1)
            dve.wait_ge(out_added, B)


def kernel(**inputs):
    import numpy as np
    import concourse.bacc as bacc
    from concourse.bass_utils import run_bass_kernel_spmd as run

    A = {k: np.asarray(v) for k, v in inputs.items()}
    a = {k[len("L0_attn_a_"):]: v for k, v in A.items() if k.startswith("L0_attn_a_")}
    r = {k[len("L0_attn_b_"):]: v for k, v in A.items() if k.startswith("L0_attn_b_")}
    f = {k[len("L0_ffn_"):]: v for k, v in A.items() if k.startswith("L0_ffn_")}

    headmask = np.kron(np.eye(HU, dtype=np.float32), np.ones((BD, NF), np.float32))
    place = np.zeros((HU, 2, BD, LQ, 2, HU, LQ), np.float32)
    for h in range(HU):
        for kind in range(2):
            for lag in range(LQ):
                place[h, kind, :, lag, kind, h, LQ - 1 - lag] = 1.0
    mask_place = np.zeros((LQ, BU, 2, HU, LQ), np.float32)
    mask_rows = np.zeros((LQ, PAD + T), np.float32)
    for w in range(LQ):
        mask_place[w, :, 0, :, w] = 1.0
        mask_rows[w, :PAD + LQ - 1 - w] = MASKED

    def columns(v, n=1):
        return np.tile(np.asarray(v).reshape(-1, 1), (n, 1))

    parts = {
        "ident": np.eye(128, dtype=np.float32),
        "mean_w": np.full((128, 1), 1.0 / C, np.float32),
        "centre_w": np.eye(128, dtype=np.float32) - np.float32(1.0 / C),
        "ones_w": np.ones((128, 128), np.float32),
        "minus_half": np.full((128, 4), -0.5, np.float32),
        "headmask": headmask,
        "fusedT": np.tile(a["strain_fused_w"].T, (HU, HU)),
        "disp": a["W_disp"].reshape(HG, HU * BD, C).transpose(1, 0, 2).reshape(HU * BD, HG * C),
        "posT": np.tile(np.concatenate([a["pos_proj_w"].T, np.zeros((BD, BD), np.float32)], 1), (1, HU)),
        "relT": a["rel_pos_emb"][::-1].T,
        "place": place.reshape(128, LQ * 32),
        "valT": a["W_val"].T,
        "wf": f["wf"].T, "uf": f["uf"].T, "wi": f["wi"].T, "ui": f["ui"].T,
        "wc": f["wc"].T, "uc": f["uc"].T, "wo": f["wo"].T, "uo": f["uo"].T,
        "rk": r["W_k"].T, "rv": r["W_v"].T, "rr": r["W_r"].T, "ro": r["W_o"].T,
        "strain_b": columns(a["strain_fused_b"], HU),
        "out_w": columns(np.concatenate([a["bond_out_w"][0], a["damage_out_w"][0]]), HU),
        "damage_b": columns(a["damage_out_b"], 128),
        "bf": columns(f["bf"]), "bi": columns(f["bi"]), "bc": columns(f["bc"]), "bo": columns(f["bo"]),
        "c0": columns(f["in_c"]),
        "td": columns(r["time_decay"]), "tf": columns(r["time_first"]),
        "mk": columns(r["time_mix_k"]), "mv": columns(r["time_mix_v"]), "mr": columns(r["time_mix_r"]),
        "mask_place": mask_place.reshape(LQ, 128), "mask_rows": mask_rows,
    }
    pack = np.zeros((128, WIDTH), np.float32)
    for name, part in parts.items():
        lo, hi = COL[name]
        pack[:part.shape[0], lo:hi] = part
    cp = np.zeros((HG, HU, 32, C), np.float32)
    cp[:, :, :HS, :] = a["c_proj_w"].T.reshape(HG, HU, HS, C)
    xT = np.ascontiguousarray(a["x"].transpose(2, 0, 1))

    nc = bacc.Bacc("TRN2", target_bir_lowering=False, num_devices=1)
    arrays = {"xT": xT, "pack": pack, "cp": cp.reshape(HG, 128, C)}
    args = [nc.dram_tensor(k, v.shape, mybir.dt.from_np(v.dtype), kind="ExternalInput").ap()
            for k, v in arrays.items()]
    args.append(nc.dram_tensor("outT", (128, B, T), F32, kind="ExternalOutput").ap())
    program(nc, *args)
    res = run(nc, [arrays], core_ids=[0])
    return np.ascontiguousarray(res.results[0]["outT"].transpose(1, 2, 0))
```
